# Optimizing a Trainium2 kernel written in Bass

```python
import numpy as np
import jax
import jax.numpy as jnp

def _softmax(x, axis=-1):
    return jax.nn.softmax(x, axis=axis)

def _gelu(x):
    return jax.nn.gelu(x, approximate=True)

def _silu(x):
    return jax.nn.silu(x)

def _sigmoid(x):
    return jax.nn.sigmoid(x)

def _layernorm(x, axis=-1, eps=1e-05):
    m = jnp.mean(x, axis=axis, keepdims=True)
    v = jnp.var(x, axis=axis, keepdims=True)
    return (x - m) / jnp.sqrt(v + eps)

def _scatter_add(tgt, idx, src, axis=0):
    return tgt.at[idx].add(src)

def _segment_sum(src, seg, n):
    return jax.ops.segment_sum(src, seg, n)
kernel_name = 'mk_perceiver_d1_seqx_r4_afb0ef'

def setup_inputs(seed: int=0):
    np.random.seed(seed)
    _w = jnp.asarray

    def _rec_inputs():
        import jax
        import jax.numpy as jnp
        _rk = jax.random.key(seed)
        x = -0.000125 + 0.9999 * jax.random.normal(jax.random.fold_in(_rk, 1), (8, 64, 512), jnp.float32)
        _lenS = 64 - jax.random.randint(jax.random.fold_in(_rk, 7), (8,), 0, max(1, 64 // 4) + 1, jnp.int32)
        _lenS2 = 1601 - jax.random.randint(jax.random.fold_in(_rk, 8), (8,), 0, max(1, 1601 // 4) + 1, jnp.int32)
        _ctx_2048P = jax.random.normal(jax.random.fold_in(_rk, 11), (8, 16, 512), jnp.float32)
        _ctx_2048c = jax.random.dirichlet(jax.random.fold_in(_rk, 511), 0.3 * jnp.ones((16,), jnp.float32), (8, 1601))
        _ctx_2048t = jnp.einsum('bsk,bkd->bsd', _ctx_2048c, _ctx_2048P)
        _ctx_2048t = _ctx_2048t * jax.lax.rsqrt(jnp.mean(jnp.square(_ctx_2048t)) + 1e-12) * 0.953939
        ctx_2048 = -0.000514642 + 1.00011 * (_ctx_2048t + 0.3 * jax.random.normal(jax.random.fold_in(_rk, 611), (8, 1601, 512), jnp.float32))
        _validS = jnp.arange(64)[None, :] < _lenS[:, None]
        _validS2 = jnp.arange(1601)[None, :] < _lenS2[:, None]
        _causal = jnp.tril(jnp.ones((64, 64), dtype=bool))
        mask_BxS2_bk0 = jnp.logical_not(jnp.broadcast_to(_validS2[:, :], (8, 1601)))
        return (x, ctx_2048, mask_BxS2_bk0)
    x, ctx_2048, mask_BxS2_bk0 = _rec_inputs()

    def _L0_xattn_setup():
        import jax, jax.numpy as jnp
        import numpy as np
        key = jax.random.key(seed)
        k1, k2, k3 = jax.random.split(key, 3)
        B, S, D, M = (8, 512, 512, 128)
        hidden_states = jax.random.normal(k1, (B, S, D), dtype=jnp.float32)
        memory_tokens = jax.random.normal(k2, (B, M, D), dtype=jnp.float32)
        memory_mask = jax.random.randint(k3, (B, M), 0, 2).astype(jnp.bool_)
        return {'hidden_states': hidden_states, 'memory_tokens': memory_tokens, 'memory_mask': memory_mask}
    _L0_xattn_all = _L0_xattn_setup()
    _L0_xattn_in = {k: v for k, v in _L0_xattn_all.items() if k in ()}
    del _L0_xattn_all

    def _L0_attn_setup():
        import jax, jax.numpy as jnp
        import numpy as np
        HIDDEN = 512
        HEADS = 16
        HEAD_DIM = HIDDEN // HEADS
        NEG = -10000000000.0
        key = jax.random.key(seed)
        k1, k2, k3 = jax.random.split(key, 3)
        x = jax.random.normal(k1, (2, 512, HIDDEN), dtype=jnp.float32)
        w_qkv = jax.random.normal(k2, (HIDDEN, 3 * HIDDEN), dtype=jnp.float32) / np.sqrt(HIDDEN)
        w_out = jax.random.normal(k3, (HIDDEN, HIDDEN), dtype=jnp.float32) / np.sqrt(HIDDEN)
        return {'x': x, 'w_qkv': w_qkv, 'w_out': w_out}
    _L0_attn_all = _L0_attn_setup()
    _L0_attn_in = {k: v for k, v in _L0_attn_all.items() if k in ('w_qkv', 'w_out')}
    del _L0_attn_all

    def _L0_ffn_setup():
        import jax, jax.numpy as jnp
        import numpy as np
        from jax import lax
        B, S, H = (1, 512, 512)
        E, I, TOP_K = (64, 128, 8)
        SHARED_I = 128
        key = jax.random.key(seed)
        ks = jax.random.split(key, 8)
        sc = 0.02
        return {'hidden_states': jax.random.normal(ks[0], (B, S, H), jnp.float32), 'router_w': jax.random.normal(ks[1], (E, H), jnp.float32) * sc, 'gate_up_proj': jax.random.normal(ks[2], (E, 2 * I, H), jnp.float32) * sc, 'down_proj': jax.random.normal(ks[3], (E, H, I), jnp.float32) * sc, 'shared_gate_w': jax.random.normal(ks[4], (SHARED_I, H), jnp.float32) * sc, 'shared_up_w': jax.random.normal(ks[5], (SHARED_I, H), jnp.float32) * sc, 'shared_down_w': jax.random.normal(ks[6], (H, SHARED_I), jnp.float32) * sc, 'shared_expert_gate_w': jax.random.normal(ks[7], (1, H), jnp.float32) * sc}
    _L0_ffn_all = _L0_ffn_setup()
    _L0_ffn_in = {k: v for k, v in _L0_ffn_all.items() if k in ('router_w', 'gate_up_proj', 'down_proj', 'shared_gate_w', 'shared_up_w', 'shared_down_w', 'shared_expert_gate_w')}
    del _L0_ffn_all
    return {'x': x, 'ctx_2048': ctx_2048, 'mask_BxS2_bk0': mask_BxS2_bk0, 'L0_attn_w_qkv': _L0_attn_in['w_qkv'], 'L0_attn_w_out': _L0_attn_in['w_out'], 'L0_ffn_router_w': _L0_ffn_in['router_w'], 'L0_ffn_gate_up_proj': _L0_ffn_in['gate_up_proj'], 'L0_ffn_down_proj': _L0_ffn_in['down_proj'], 'L0_ffn_shared_gate_w': _L0_ffn_in['shared_gate_w'], 'L0_ffn_shared_up_w': _L0_ffn_in['shared_up_w'], 'L0_ffn_shared_down_w': _L0_ffn_in['shared_down_w'], 'L0_ffn_shared_expert_gate_w': _L0_ffn_in['shared_expert_gate_w']}

def reference(x, ctx_2048, mask_BxS2_bk0, L0_attn_w_qkv, L0_attn_w_out, L0_ffn_router_w, L0_ffn_gate_up_proj, L0_ffn_down_proj, L0_ffn_shared_gate_w, L0_ffn_shared_up_w, L0_ffn_shared_down_w, L0_ffn_shared_expert_gate_w):
    import jax
    import jax.numpy as jnp

    def _L0_xattn_ref(hidden_states, memory_tokens, memory_mask):
        import jax, jax.numpy as jnp
        import numpy as np
        B, S, D = hidden_states.shape
        scale = 1.0 / jnp.sqrt(jnp.asarray(D, hidden_states.dtype))
        scores = jnp.einsum('bsd,bmd->bsm', hidden_states, memory_tokens) * scale
        neg_inf = jnp.asarray(-1e+30, scores.dtype)
        scores = jnp.where(memory_mask[:, None, :], scores, neg_inf)
        attn = jax.nn.softmax(scores, axis=-1)
        readout = jnp.einsum('bsm,bmd->bsd', attn, memory_tokens)
        valid_b = jnp.any(memory_mask, axis=-1)
        out = jnp.where(valid_b[:, None, None], readout, jnp.zeros_like(readout))
        return out

    def _L0_attn_ref(x, w_qkv, w_out):
        import jax, jax.numpy as jnp
        import numpy as np
        HIDDEN = 512
        HEADS = 16
        HEAD_DIM = HIDDEN // HEADS
        NEG = -10000000000.0
        b, s, _ = x.shape
        qkv = x @ w_qkv
        qkv = qkv.reshape(b, s, 3, HEADS, HEAD_DIM)
        q, k, v = (qkv[:, :, 0], qkv[:, :, 1], qkv[:, :, 2])
        scale = jnp.sqrt(jnp.float32(HEAD_DIM)).astype(x.dtype)
        q = q / scale
        scores = jnp.einsum('bqhd,bkhd->bhqk', q, k)
        causal_mask = jnp.arange(s)[:, None] >= jnp.arange(s)[None, :]
        scores = jnp.where(causal_mask[None, None], scores, NEG)
        attn = jax.nn.softmax(scores, axis=-1)
        out = jnp.einsum('bhqk,bkhd->bqhd', attn, v).reshape(b, s, HIDDEN)
        return out @ w_out

    def _L0_ffn_ref(hidden_states, router_w, gate_up_proj, down_proj, shared_gate_w, shared_up_w, shared_down_w, shared_expert_gate_w):
        import jax, jax.numpy as jnp
        import numpy as np
        from jax import lax
        B, S, H = (1, 512, 512)
        E, I, TOP_K = (64, 128, 8)
        SHARED_I = 128
        b, s, h_dim = hidden_states.shape
        h = hidden_states.reshape(-1, h_dim)
        T = h.shape[0]
        shared = jnp.dot(jax.nn.silu(jnp.dot(h, shared_gate_w.T)) * jnp.dot(h, shared_up_w.T), shared_down_w.T)
        shared = jax.nn.sigmoid(jnp.dot(h, shared_expert_gate_w.T)) * shared
        logits = jnp.dot(h, router_w.T)
        probs = jax.nn.softmax(logits.astype(jnp.float32), axis=-1)
        top_vals, top_idx = lax.top_k(probs, TOP_K)
        top_vals = top_vals / jnp.sum(top_vals, axis=-1, keepdims=True)
        top_vals = top_vals.astype(h.dtype)
        comb = jnp.zeros((T, E), h.dtype).at[jnp.arange(T)[:, None], top_idx].add(top_vals)

        def body(acc, xs):
            wgu, wd, w_e = xs
            g, u = jnp.split(jnp.dot(h, wgu.T), 2, axis=-1)
            eo = jnp.dot(jax.nn.silu(g) * u, wd.T)
            return (acc + eo * w_e[:, None], None)
        expert_out, _ = lax.scan(body, jnp.zeros_like(h), (gate_up_proj, down_proj, comb.T))
        return (expert_out + shared).reshape(b, s, h_dim)
    x = x + _L0_xattn_ref(_layernorm(x, axis=-1), ctx_2048, mask_BxS2_bk0)
    x = x + _L0_attn_ref(_layernorm(x, axis=-1), L0_attn_w_qkv, L0_attn_w_out)
    x = x + _L0_ffn_ref(_layernorm(x, axis=-1), L0_ffn_router_w, L0_ffn_gate_up_proj, L0_ffn_down_proj, L0_ffn_shared_gate_w, L0_ffn_shared_up_w, L0_ffn_shared_down_w, L0_ffn_shared_expert_gate_w)
    return x

_drawn_inputs = setup_inputs


def setup_inputs(seed=0):
    import zlib

    import numpy as np

    out = dict(_drawn_inputs(seed))
    spreads = {}
    factors = {'L0_ffn_router_w': 7.271,
     'L0_ffn_gate_up_proj': 6.058,
     'L0_ffn_down_proj': 6.141,
     'L0_ffn_shared_gate_w': 5.861,
     'L0_ffn_shared_up_w': 5.747,
     'L0_ffn_shared_down_w': 5.79,
     'L0_ffn_shared_expert_gate_w': 8.0}
    for name, (base, spread) in spreads.items():
        noise = np.random.default_rng([zlib.crc32(name.encode()), seed]).standard_normal(out[name].shape)
        drawn = base * np.exp(spread * noise) if base else spread * noise
        out[name] = jnp.asarray(drawn.astype(out[name].dtype))
    for name, factor in factors.items():
        out[name] = (out[name] * factor).astype(out[name].dtype)
    return out
```

```python
from contextlib import ExitStack

import concourse.bass as bass
from concourse import mybir

ALU = mybir.AluOpType
ACT = mybir.ActivationFunctionType
F32 = mybir.dt.float32
BF16 = mybir.dt.bfloat16
U8 = mybir.dt.uint8
AX_X = mybir.AxisListType.X

P = 128
S = 64
HB = P // S
NEG_MASK = 1.0e30
NEG_CAUSAL = 1.0e10
EPS = 1e-5


def build_program(nc, x, ctx_rows, ctx_cols, mask, w_qkv, w_out, w_router, w_shared, w_expert, out):
    T, D = x.shape
    NT = T // P
    KD = D // P
    B, NCH = ctx_rows.shape[:2]
    M = NCH * P
    HEADS, DH = 16, D // 16
    RG = P // DH
    NG = HEADS // RG
    E = w_expert.shape[0]
    I = P
    SC_CTX = float(D) ** -0.5
    SC_HEAD = float(DH) ** -0.5
    EO = E + 1
    RING = 4

    with ExitStack() as st:
        def sb(name, shape, dt=F32):
            return st.enter_context(nc.sbuf_tensor(name, shape, dt))

        def sem(name):
            return st.enter_context(nc.semaphore(name))

        bank = st.enter_context(nc.psum_tensor("bank", [P, 8, 512], F32))

        ident = sb("ident", [P, P])
        causal = sb("causal", [P, HEADS, S])
        xt = sb("xt", [P, NT, D])
        xn = sb("xn", [P, NT, D])
        xT = sb("xT", [P, KD, T])
        stats = sb("stats", [P, NT, 6])
        mv = sb("mv", [P, NT, 2])
        var = sb("var", [P, NT])
        std = sb("std", [P, NT])
        rstd = sb("rstd", [P, NT])
        wqkv_sb = sb("wqkv_sb", [P, KD, 3 * D])
        wout_sb = sb("wout_sb", [P, KD, D])
        wr_sb = sb("wr_sb", [P, KD, EO])
        wsh_sb = sb("wsh_sb", [P, KD * 2 * I + D])

        def norm_tiles(vec, step, std_ready, xn_ready):
            for j in range(NT):
                nc.vector.bn_stats(stats[:, j], xt[:, j]).then_inc(step, 1)
            vec.wait_ge(step, NT)
            for j in range(NT):
                nc.vector.bn_aggr(mv[:, j], stats[:, j]).then_inc(step, 1)
            vec.wait_ge(step, 2 * NT)
            nc.vector.tensor_scalar(var[:], mv[:, :, 1], EPS, None, ALU.add).then_inc(step, 1)
            vec.wait_ge(std_ready, 1)
            nc.vector.reciprocal(rstd[:], std[:]).then_inc(step, 1)
            vec.wait_ge(step, 2 * NT + 2)
            for j in range(NT):
                nc.vector.tensor_scalar(xn[:, j], xt[:, j], mv[:, j, 0:1], rstd[:, j:j + 1],
                                        ALU.subtract, ALU.mult).then_inc(xn_ready, 1)

        with ExitStack() as ph:
            def sbp(name, shape, dt=F32):
                return ph.enter_context(nc.sbuf_tensor(name, shape, dt))

            def semp(name):
                return ph.enter_context(nc.semaphore(name))

            cT = sbp("cT", [P, NCH, KD * P])
            cR = sbp("cR", [P, NCH, D])
            mrow = sbp("mrow", [P, NT, M], U8)
            bias = sbp("bias", [P, M])
            prob = sbp("prob", [P, M])
            probT = sbp("probT", [P, NCH, P])
            rmax = sbp("rmax", [P, NT])
            nmax = sbp("nmax", [P, NT])
            rsum = sbp("rsum", [P, NT])
            rinv = sbp("rinv", [P, NT])
            anyv = sbp("anyv", [P, NT])
            gain = sbp("gain", [P, NT])

            ld_x, ld_mask = semp("ld_x"), semp("ld_mask")
            ld_w = sem("ld_w")
            ld_cT = [semp(f"ld_cT{c}") for c in range(NCH)]
            ld_cR = [semp(f"ld_cR{c}") for c in range(NCH)]
            ident_ready, ident_zero = semp("ident_ready"), semp("ident_zero")
            causal_zero, causal_ready = semp("causal_zero"), semp("causal_ready")
            ln_step = semp("ln_step")
            std_ready = semp("std_ready")
            xn_ready = semp("xn_ready")
            xT_done, xT_ready = semp("xT_done"), semp("xT_ready")
            scores_done = semp("scores_done")
            bias_ready = semp("bias_ready")
            anyv_ready = semp("anyv_ready")
            scores_read = semp("scores_read")
            max_ready, nmax_ready = semp("max_ready"), semp("nmax_ready")
            exp_ready = semp("exp_ready")
            pT_done, pT_copied = semp("pT_done"), semp("pT_copied")
            pv_done = semp("pv_done")
            rinv_ready, gain_ready = semp("rinv_ready"), semp("gain_ready")
            x1_ready = semp("x1_ready")
            NPT = -(-NCH // 4)

            with nc.Block() as block:
                @block.sync
                def _(sp):
                    sp.dma_start(xt[:], x.rearrange("(t p) d -> p t d", p=P)).then_inc(ld_x, 16)
                    for half in range(HB):
                        sp.dma_start(mrow[half * S:(half + 1) * S],
                                     mask.rearrange("(j h) m -> h j m", h=HB)[half].partition_broadcast(S)
                                     ).then_inc(ld_mask, 16)
                    for b in range(B):
                        for c in range(NCH):
                            if b:
                                sp.wait_ge(scores_done, NCH * (b - 1) + c + 1)
                            sp.dma_start(cT[:, c], ctx_cols[b, c]).then_inc(ld_cT[c], 16)

                @block.gpsimd
                def _(pool):
                    nc.gpsimd.memset(ident[:], 0.0).then_inc(ident_zero, 1)
                    pool.wait_ge(ident_zero, 1)
                    nc.gpsimd.affine_select(out=ident[:], in_=ident[:], compare_op=ALU.not_equal, fill=1.0,
                                            base=0, pattern=[[-1, P]], channel_multiplier=1).then_inc(ident_ready, 1)
                    for half in range(HB):
                        nc.gpsimd.memset(causal[half * S:(half + 1) * S], 0.0).then_inc(causal_zero, 1)
                        pool.wait_ge(causal_zero, half + 1)
                        nc.gpsimd.affine_select(out=causal[half * S:(half + 1) * S],
                                                in_=causal[half * S:(half + 1) * S],
                                                compare_op=ALU.is_ge, fill=-NEG_CAUSAL, base=0,
                                                pattern=[[0, HEADS], [-1, S]],
                                                channel_multiplier=1).then_inc(causal_ready, 1)
                    pool.wait_ge(causal_ready, HB)
                    pool.wait_ge(ld_mask, 16 * HB)
                    for j in range(NT):
                        if j:
                            pool.wait_ge(scores_read, j)
                        nc.gpsimd.tensor_scalar(bias[:], mrow[:, j], -1.0, NEG_MASK,
                                                ALU.add, ALU.mult).then_inc(bias_ready, 1)

                @block.scalar
                def _(act):
                    act.dma_start(wqkv_sb[:], w_qkv).then_inc(ld_w, 16)
                    act.dma_start(wout_sb[:], w_out).then_inc(ld_w, 16)
                    act.dma_start(wr_sb[:], w_router).then_inc(ld_w, 16)
                    act.dma_start(wsh_sb[:], w_shared).then_inc(ld_w, 16)
                    act.wait_ge(ln_step, 2 * NT + 1)
                    nc.scalar.activation(std[:], var[:], ACT.Sqrt).then_inc(std_ready, 1)

                    def load_rows(b):
                        for c in range(NCH):
                            if b:
                                act.wait_ge(pv_done, NCH * (b - 1) + c + 1)
                            act.dma_start(cR[:, c], ctx_rows[b, c]).then_inc(ld_cR[c], 16)

                    load_rows(0)
                    for j in range(NT):
                        act.wait_ge(xT_done, j + 1)
                        nc.scalar.activation(xT[:, :, j * P:(j + 1) * P],
                                             bank[:, 6 + j % 2].rearrange("p (k t) -> p k t", k=KD),
                                             ACT.Copy).then_inc(xT_ready, 1)
                    for j in range(NT):
                        act.wait_ge(nmax_ready, j + 1)
                        nc.scalar.activation(prob[:], prob[:], ACT.Exp, bias=nmax[:, j:j + 1],
                                             accum_out=rsum[:, j:j + 1]).then_inc(exp_ready, 1)
                        for g in range(NPT):
                            act.wait_ge(pT_done, NPT * j + g + 1)
                            n = min(4, NCH - 4 * g)
                            nc.scalar.activation(probT[:, 4 * g:4 * g + n],
                                                 bank[:, 4 + g % 2, 0:n * P].rearrange("p (c q) -> p c q", c=n),
                                                 ACT.Copy).then_inc(pT_copied, 1)
                        load_rows(HB * j + 1)
                        if j + 1 < NT:
                            load_rows(HB * j + 2)

                @block.vector
                def _(vec):
                    vec.wait_ge(ld_x, 16)
                    norm_tiles(vec, ln_step, std_ready, xn_ready)
                    vec.wait_ge(ld_mask, 16 * HB)
                    nc.vector.tensor_reduce(anyv[:], mrow[:], AX_X, ALU.max).then_inc(anyv_ready, 1)
                    vec.wait_ge(anyv_ready, 1)
                    for j in range(NT):
                        vec.wait_ge(scores_done, NCH * HB * (j + 1))
                        vec.wait_ge(bias_ready, j + 1)
                        if j:
                            vec.wait_ge(pT_done, NPT * j)
                        nc.vector.scalar_tensor_tensor(
                            out=prob[:], in0=bank[:, 0:4].rearrange("p b n -> p (b n)")[:, 0:M],
                            scalar=SC_CTX, in1=bias[:], op0=ALU.mult, op1=ALU.add).then_inc(scores_read, 1)
                        vec.wait_ge(scores_read, j + 1)
                        nc.vector.tensor_reduce(rmax[:, j:j + 1], prob[:], AX_X, ALU.max).then_inc(max_ready, 1)
                        vec.wait_ge(max_ready, j + 1)
                        nc.vector.tensor_scalar(nmax[:, j:j + 1], rmax[:, j:j + 1], -1.0, None,
                                                ALU.mult).then_inc(nmax_ready, 1)
                        vec.wait_ge(exp_ready, j + 1)
                        nc.vector.reciprocal(rinv[:, j:j + 1], rsum[:, j:j + 1]).then_inc(rinv_ready, 1)
                        vec.wait_ge(rinv_ready, j + 1)
                        nc.vector.tensor_tensor(gain[:, j:j + 1], rinv[:, j:j + 1], anyv[:, j:j + 1],
                                                ALU.mult).then_inc(gain_ready, 1)
                        vec.wait_ge(gain_ready, j + 1)
                        vec.wait_ge(pv_done, NCH * HB * (j + 1))
                        nc.vector.scalar_tensor_tensor(out=xt[:, j], in0=bank[:, 6 + j % 2], scalar=gain[:, j:j + 1],
                                                       in1=xt[:, j], op0=ALU.mult, op1=ALU.add).then_inc(x1_ready, 1)

                @block.tensor
                def _(pe):
                    pe.wait_ge(ident_ready, 1)
                    for j in range(NT):
                        pe.wait_ge(xn_ready, j + 1)
                        if j >= 2:
                            pe.wait_ge(xT_ready, j - 1)
                        for k in range(KD):
                            ins = nc.tensor.transpose(bank[:, 6 + j % 2, k * P:(k + 1) * P],
                                                      xn[:, j, k * P:(k + 1) * P], ident[:])
                        ins.then_inc(xT_done, 1)
                    pe.wait_ge(xT_ready, NT)

                    def scores(j):
                        if j:
                            pe.wait_ge(scores_read, j)
                        for half in range(HB):
                            b = HB * j + half
                            tok = slice(b * S, (b + 1) * S)
                            for c in range(NCH):
                                pe.wait_ge(ld_cT[c], 16 * (b + 1))
                                for k in range(KD):
                                    ins = nc.tensor.matmul(
                                        bank[half * S:(half + 1) * S, c // 4, (c % 4) * P:(c % 4 + 1) * P],
                                        xT[:, k, tok], cT[:, c, k * P:(k + 1) * P],
                                        start=(k == 0), stop=(k == KD - 1))
                                ins.then_inc(scores_done, 1)

                    def attend(j):
                        pe.wait_ge(exp_ready, j + 1)
                        for g in range(NPT):
                            if NPT * j + g >= 2:
                                pe.wait_ge(pT_copied, NPT * j + g - 1)
                            for c in range(4 * g, min(4 * g + 4, NCH)):
                                ins = nc.tensor.transpose(bank[:, 4 + g % 2, (c % 4) * P:(c % 4 + 1) * P],
                                                          prob[:, c * P:(c + 1) * P], ident[:])
                            ins.then_inc(pT_done, 1)
                        if j >= 2:
                            pe.wait_ge(x1_ready, j - 1)
                        for half in range(HB):
                            b = HB * j + half
                            for c in range(NCH):
                                if half == 0:
                                    pe.wait_ge(pT_copied, NPT * j + c // 4 + 1)
                                pe.wait_ge(ld_cR[c], 16 * (b + 1))
                                nc.tensor.matmul(bank[half * S:(half + 1) * S, 6 + j % 2],
                                                 probT[:, c, half * S:(half + 1) * S], cR[:, c],
                                                 start=(c == 0), stop=(c == NCH - 1)).then_inc(pv_done, 1)

                    scores(0)
                    for j in range(NT):
                        if j + 1 < NT:
                            scores(j + 1)
                        attend(j)

        with ExitStack() as ph:
            def sbp(name, shape, dt=F32):
                return ph.enter_context(nc.sbuf_tensor(name, shape, dt))

            def semp(name):
                return ph.enter_context(nc.semaphore(name))

            qkT = sbp("qkT", [P, 2 * NG, T])
            v = sbp("v", [P, NT, D])
            vswap = sbp("vswap", [P, NT, D])
            sc = sbp("sc", [P, 2, HEADS, S])
            pT = sbp("pT", [P, 2, HEADS // 2, P])
            o = sbp("o", [P, NT, D])
            oT = sbp("oT", [P, KD, T])
            hmax = sbp("hmax", [P, NT, HEADS])
            hsum = sbp("hsum", [P, NT, HEADS])
            hinv = sbp("hinv", [P, NT, HEADS])

            b_ln, b_std, b_xn = semp("b_ln"), semp("b_std"), semp("b_xn")
            b_xT_done, b_xT_ready = semp("b_xT_done"), semp("b_xT_ready")
            qk_done, qk_ready = semp("qk_done"), semp("qk_ready")
            v_done, v_ready, vswap_ready = semp("v_done"), semp("v_ready"), semp("vswap_ready")
            hs_done, hs_read = semp("hs_done"), semp("hs_read")
            hmax_ready, sub_ready, hexp_ready = semp("hmax_ready"), semp("sub_ready"), semp("hexp_ready")
            hsum_ready, hinv_ready = semp("hsum_ready"), semp("hinv_ready")
            hpT_done, hpT_copied = semp("hpT_done"), semp("hpT_copied")
            ho_done, o_ready = semp("ho_done"), semp("o_ready")
            oT_done, oT_ready = semp("oT_done"), semp("oT_ready")
            y_done, x2_ready = semp("y_done"), semp("x2_ready")

            with nc.Block() as block:
                @block.sync
                def _(sp):
                    for half in range(HB):
                        sp.wait_ge(v_ready, NT)
                        lo, hi = half * S, (1 - half) * S
                        sp.dma_start(vswap[lo:lo + S], v[hi:hi + S]).then_inc(vswap_ready, 16)

                @block.vector
                def _(vec):
                    norm_tiles(vec, b_ln, b_std, b_xn)
                    for t in range(NT):
                        vec.wait_ge(v_done, t + 1)
                        nc.vector.tensor_copy(v[:, t], bank[:, 4 + t]).then_inc(v_ready, 1)

                    def softmax(j):
                        buf = sc[:, j % 2]
                        vec.wait_ge(hs_done, j + 1)
                        if j >= 2:
                            vec.wait_ge(hpT_done, 2 * (j - 1))
                        nc.vector.scalar_tensor_tensor(
                            out=buf.rearrange("p (r g) k -> p r g k", r=RG),
                            in0=bank[:, 0:4, 0:NG * S].rearrange("p r (g k) -> p r g k", g=NG), scalar=SC_HEAD,
                            in1=causal[:].rearrange("p (r g) k -> p r g k", r=RG), op0=ALU.mult, op1=ALU.add).then_inc(hs_read, 1)
                        vec.wait_ge(hs_read, j + 1)
                        nc.vector.tensor_reduce(hmax[:, j], buf, AX_X, ALU.max).then_inc(hmax_ready, 1)
                        vec.wait_ge(hmax_ready, j + 1)
                        nc.vector.tensor_tensor(buf, buf, hmax[:, j].unsqueeze(2).broadcast_to([P, HEADS, S]),
                                                ALU.subtract).then_inc(sub_ready, 1)

                    def finish(j):
                        vec.wait_ge(hexp_ready, j + 1)
                        nc.vector.tensor_reduce(hsum[:, j], sc[:, j % 2], AX_X, ALU.add).then_inc(hsum_ready, 1)
                        vec.wait_ge(hsum_ready, j + 1)
                        nc.vector.reciprocal(hinv[:, j], hsum[:, j]).then_inc(hinv_ready, 1)
                        vec.wait_ge(hinv_ready, j + 1)
                        vec.wait_ge(ho_done, j + 1)
                        for hh in range(2):
                            ov = o[:, j].rearrange("p (gp hh r d) -> p hh r gp d", gp=NG // 2, hh=2, r=RG)[:, hh]
                            iv = hinv[:, j].rearrange("p (r gp hh) -> p hh r gp", r=RG, hh=2)[:, hh]
                            nc.vector.tensor_tensor(
                                ov, bank[:, 6 + hh, 0:HEADS // 2 * DH].rearrange("p (r gp d) -> p r gp d", r=RG, gp=NG // 2),
                                iv.unsqueeze(3).broadcast_to([P, RG, NG // 2, DH]), ALU.mult).then_inc(o_ready, 1)

                    softmax(0)
                    for j in range(NT):
                        if j + 1 < NT:
                            softmax(j + 1)
                        finish(j)
                    for j in range(NT):
                        vec.wait_ge(y_done, j + 1)
                        nc.vector.tensor_tensor(xt[:, j], bank[:, 4 + j], xt[:, j], ALU.add).then_inc(x2_ready, 1)

                @block.scalar
                def _(act):
                    act.wait_ge(b_ln, 2 * NT + 1)
                    nc.scalar.activation(std[:], var[:], ACT.Sqrt).then_inc(b_std, 1)
                    for j in range(NT):
                        act.wait_ge(b_xT_done, j + 1)
                        nc.scalar.activation(xT[:, :, j * P:(j + 1) * P],
                                             bank[:, j].rearrange("p (k t) -> p k t", k=KD),
                                             ACT.Copy).then_inc(b_xT_ready, 1)
                    for g in range(2 * NG):
                        act.wait_ge(qk_done, g + 1)
                        nc.scalar.activation(qkT[:, g], bank[:, g % 4], ACT.Copy).then_inc(qk_ready, 1)

                    def copies(j):
                        for n in range(2):
                            act.wait_ge(hpT_done, 2 * j + n + 1)
                            if j >= 2:
                                act.wait_ge(ho_done, j - 1)
                            nc.scalar.activation(pT[:, j % 2, 4 * n:4 * n + 4],
                                                 bank[:, 4 + n].rearrange("p (c q) -> p c q", c=4),
                                                 ACT.Copy).then_inc(hpT_copied, 1)

                    for j in range(NT):
                        act.wait_ge(sub_ready, j + 1)
                        nc.scalar.activation(sc[:, j % 2], sc[:, j % 2], ACT.Exp).then_inc(hexp_ready, 1)
                        if j:
                            copies(j - 1)
                    copies(NT - 1)
                    for j in range(NT):
                        act.wait_ge(oT_done, j + 1)
                        nc.scalar.activation(oT[:, :, j * P:(j + 1) * P],
                                             bank[:, j].rearrange("p (k t) -> p k t", k=KD),
                                             ACT.Copy).then_inc(oT_ready, 1)

                @block.tensor
                def _(pe):
                    for j in range(NT):
                        pe.wait_ge(b_xn, j + 1)
                        for k in range(KD):
                            ins = nc.tensor.transpose(bank[:, j, k * P:(k + 1) * P],
                                                      xn[:, j, k * P:(k + 1) * P], ident[:])
                        ins.then_inc(b_xT_done, 1)
                    pe.wait_ge(ld_w, 16 * 4)
                    for t in range(NT):
                        pe.wait_ge(b_xT_ready, t + 1)
                        for k in range(KD):
                            ins = nc.tensor.matmul(bank[:, 4 + t], xT[:, k, t * P:(t + 1) * P],
                                                   wqkv_sb[:, k, 2 * D:3 * D], start=(k == 0), stop=(k == KD - 1))
                        ins.then_inc(v_done, 1)
                    for g in range(2 * NG):
                        if g >= 4:
                            pe.wait_ge(qk_ready, g - 3)
                        for k in range(KD):
                            ins = nc.tensor.matmul(bank[:, g % 4], wqkv_sb[:, k, g * P:(g + 1) * P], xT[:, k],
                                                   start=(k == 0), stop=(k == KD - 1))
                        ins.then_inc(qk_done, 1)

                    def scores(j):
                        if j == 0:
                            pe.wait_ge(qk_ready, 2 * NG)
                        else:
                            pe.wait_ge(hs_read, j)
                        for g in range(NG):
                            for r in range(RG):
                                rows = slice(r * DH, (r + 1) * DH)
                                for half in range(HB):
                                    tok = slice((HB * j + half) * S, (HB * j + half + 1) * S)
                                    ins = nc.tensor.matmul(bank[half * S:(half + 1) * S, r, g * S:(g + 1) * S],
                                                           qkT[rows, g, tok], qkT[rows, NG + g, tok],
                                                           start=True, stop=True, tile_position=(r * DH, half * S))
                        ins.then_inc(hs_done, 1)

                    def attend(j):
                        pe.wait_ge(hexp_ready, j + 1)
                        for n in range(2):
                            if j == 0:
                                pe.wait_ge(v_ready, NT)
                            else:
                                pe.wait_ge(hpT_copied, 2 * (j - 1) + n + 1)
                            for c in range(4):
                                tp = 4 * n + c
                                ins = nc.tensor.transpose(
                                    bank[:, 4 + n, c * P:(c + 1) * P],
                                    sc[:, j % 2, 2 * tp:2 * tp + 2].rearrange("p h k -> p (h k)"), ident[:])
                            ins.then_inc(hpT_done, 1)
                        pe.wait_ge(vswap_ready, 16 * HB)
                        if j:
                            pe.wait_ge(o_ready, 2 * j)
                        for n in range(2):
                            pe.wait_ge(hpT_copied, 2 * j + n + 1)
                            for c in range(4):
                                tp = 4 * n + c
                                r, gp = tp // (NG // 2), tp % (NG // 2)
                                for hh in range(2):
                                    h = RG * (2 * gp + hh) + r
                                    for half in range(HB):
                                        vv = v if half == hh else vswap
                                        ins = nc.tensor.matmul(
                                            bank[half * S:(half + 1) * S, 6 + hh, tp * DH:(tp + 1) * DH],
                                            pT[hh * S:(hh + 1) * S, j % 2, tp, half * S:(half + 1) * S],
                                            vv[hh * S:(hh + 1) * S, j, h * DH:(h + 1) * DH],
                                            start=True, stop=True, tile_position=(hh * S, half * S))
                        ins.then_inc(ho_done, 1)

                    scores(0)
                    for j in range(NT):
                        if j + 1 < NT:
                            scores(j + 1)
                        attend(j)
                    pe.wait_ge(hs_read, NT)
                    for j in range(NT):
                        pe.wait_ge(o_ready, 2 * (j + 1))
                        for k in range(KD):
                            ins = nc.tensor.transpose(bank[:, j, k * P:(k + 1) * P],
                                                      o[:, j, k * P:(k + 1) * P], ident[:])
                        ins.then_inc(oT_done, 1)
                    for j in range(NT):
                        pe.wait_ge(oT_ready, j + 1)
                        for k in range(KD):
                            ins = nc.tensor.matmul(bank[:, 4 + j], oT[:, k, j * P:(j + 1) * P], wout_sb[:, k],
                                                   start=(k == 0), stop=(k == KD - 1))
                        ins.then_inc(y_done, 1)

        with ExitStack() as ph:
            def sbp(name, shape, dt=F32):
                return ph.enter_context(nc.sbuf_tensor(name, shape, dt))

            def semp(name):
                return ph.enter_context(nc.semaphore(name))

            WE = KD * 2 * I + D
            ring = sbp("ring", [P, RING, WE])
            logit = sbp("logit", [P, NT, EO])
            top8 = sbp("top8", [P, NT, 8])
            rest = sbp("rest", [P, NT, E])
            lexp = sbp("lexp", [P, NT, E])
            nl = sbp("nl", [P, NT])
            wsum = sbp("wsum", [P, NT])
            winv = sbp("winv", [P, NT])
            comb = sbp("comb", [P, NT, E])
            sgate = sbp("sgate", [P, NT])
            sil = sbp("sil", [P, 2, T])
            hid = sbp("hid", [P, 2, T])
            acc = sbp("acc", [P, NT, D])

            c_ln, c_std, c_xn = semp("c_ln"), semp("c_std"), semp("c_xn")
            c_xT_done, c_xT_ready = semp("c_xT_done"), semp("c_xT_ready")
            logit_done, logit_ready = semp("logit_done"), semp("logit_ready")
            top_step, lexp_ready, comb_ready = semp("top_step"), semp("lexp_ready"), semp("comb_ready")
            sgate_ready = semp("sgate_ready")
            gu_done, sil_ready, hid_ready = semp("gu_done"), semp("sil_ready"), semp("hid_ready")
            eo_done, acc_ready = semp("eo_done"), semp("acc_ready")
            ld_e = [semp(f"ld_e{r}") for r in range(RING)]
            stored = semp("stored")

            def gate_w(w, part, k):
                return w[:, (k * 2 + part) * I:(k * 2 + part + 1) * I]

            def down_w(w):
                return w[:, KD * 2 * I:WE]

            with nc.Block() as block:
                @block.sync
                def _(sp):
                    for r in range(RING):
                        sp.dma_start(ring[:, r], w_expert[r]).then_inc(ld_e[r], 16)
                    with sp.Fori(1, E // RING) as q:
                        for r in range(RING):
                            sp.wait_ge(eo_done, q * (NT * RING) + NT * (r - RING + 2))
                            sp.dma_start(ring[:, r], w_expert[bass.ds(q * RING + r, 1)].rearrange("a p n -> p (a n)")
                                         ).then_inc(ld_e[r], 16)
                    sp.wait_ge(acc_ready, NT * (E + 1))
                    sp.dma_start(out.rearrange("(t p) d -> p t d", p=P), acc[:]).then_inc(stored, 16)
                    sp.wait_ge(stored, 16)

                @block.vector
                def _(vec):
                    norm_tiles(vec, c_ln, c_std, c_xn)
                    vec.wait_ge(logit_done, NT)
                    nc.vector.tensor_copy(logit[:], bank[:, 6, 0:NT * EO].rearrange("p (t e) -> p t e", t=NT)
                                          ).then_inc(logit_ready, 1)
                    vec.wait_ge(logit_ready, 1)
                    for j in range(NT):
                        nc.vector.max(top8[:, j], logit[:, j, 0:E]).then_inc(top_step, 1)
                    vec.wait_ge(top_step, NT)
                    nc.vector.tensor_scalar(nl[:], top8[:, :, 0], -1.0, None, ALU.mult).then_inc(top_step, 1)
                    for j in range(NT):
                        nc.vector.match_replace(rest[:, j], top8[:, j], logit[:, j, 0:E], -3.0e38).then_inc(top_step, 1)
                    vec.wait_ge(top_step, 2 * NT + 1)
                    nc.vector.tensor_tensor(rest[:], rest[:], logit[:, :, 0:E], ALU.not_equal).then_inc(top_step, 1)
                    vec.wait_ge(top_step, 2 * NT + 2)
                    vec.wait_ge(lexp_ready, NT)
                    nc.vector.tensor_tensor(lexp[:], rest[:], lexp[:], ALU.mult).then_inc(top_step, 1)
                    vec.wait_ge(top_step, 2 * NT + 3)
                    nc.vector.tensor_reduce(wsum[:], lexp[:], AX_X, ALU.add).then_inc(top_step, 1)
                    vec.wait_ge(top_step, 2 * NT + 4)
                    nc.vector.reciprocal(winv[:], wsum[:]).then_inc(top_step, 1)
                    vec.wait_ge(top_step, 2 * NT + 5)
                    for j in range(NT):
                        nc.vector.tensor_scalar(comb[:, j], lexp[:, j], winv[:, j:j + 1], None,
                                                ALU.mult).then_inc(comb_ready, 1)

                    def gate(i, r):
                        vec.wait_ge(sil_ready, i + 1)
                        nc.vector.tensor_tensor(hid[:, r % 2], sil[:, r % 2], bank[:, 2 * (r % 2) + 1],
                                                ALU.mult).then_inc(hid_ready, 1)

                    gate(0, 0)
                    vec.wait_ge(sgate_ready, 1)
                    for t in range(NT):
                        vec.wait_ge(eo_done, t + 1)
                        nc.vector.scalar_tensor_tensor(out=acc[:, t], in0=bank[:, 4 + t], scalar=sgate[:, t:t + 1],
                                                       in1=xt[:, t], op0=ALU.mult, op1=ALU.add).then_inc(acc_ready, 1)
                    vec.wait_ge(comb_ready, NT)
                    with vec.Fori(0, E // RING) as q:
                        for r in range(RING):
                            gate(q * RING + (r + 1), r + 1)
                            for t in range(NT):
                                vec.wait_ge(acc_ready, q * (NT * RING) + (NT * r + t + 1))
                                vec.wait_ge(eo_done, q * (NT * RING) + (NT * (r + 1) + t + 1))
                                nc.vector.scalar_tensor_tensor(
                                    out=acc[:, t], in0=bank[:, 4 + t], scalar=comb[:, t, bass.ds(q * RING + r, 1)],
                                    in1=acc[:, t], op0=ALU.mult, op1=ALU.add).then_inc(acc_ready, 1)

                @block.scalar
                def _(act):
                    act.wait_ge(c_ln, 2 * NT + 1)
                    nc.scalar.activation(std[:], var[:], ACT.Sqrt).then_inc(c_std, 1)
                    for j in range(NT):
                        act.wait_ge(c_xT_done, j + 1)
                        nc.scalar.activation(xT[:, :, j * P:(j + 1) * P],
                                             bank[:, j].rearrange("p (k t) -> p k t", k=KD),
                                             ACT.Copy).then_inc(c_xT_ready, 1)
                    act.wait_ge(top_step, NT + 1)
                    for j in range(NT):
                        nc.scalar.activation(lexp[:, j], logit[:, j, 0:E], ACT.Exp,
                                             bias=nl[:, j:j + 1]).then_inc(lexp_ready, 1)
                    nc.scalar.activation(sgate[:], logit[:, :, E], ACT.Sigmoid).then_inc(sgate_ready, 1)

                    def silu(i, r):
                        act.wait_ge(gu_done, i + 1)
                        nc.scalar.activation(sil[:, r % 2], bank[:, 2 * (r % 2)], ACT.Silu).then_inc(sil_ready, 1)

                    silu(0, 0)
                    with act.Fori(0, E // RING) as q:
                        for r in range(RING):
                            silu(q * RING + (r + 1), r + 1)

                @block.tensor
                def _(pe):
                    for j in range(NT):
                        pe.wait_ge(c_xn, j + 1)
                        for k in range(KD):
                            ins = nc.tensor.transpose(bank[:, j, k * P:(k + 1) * P],
                                                      xn[:, j, k * P:(k + 1) * P], ident[:])
                        ins.then_inc(c_xT_done, 1)
                    for j in range(NT):
                        pe.wait_ge(c_xT_ready, j + 1)
                        for k in range(KD):
                            ins = nc.tensor.matmul(bank[:, 6, j * EO:(j + 1) * EO], xT[:, k, j * P:(j + 1) * P],
                                                   wr_sb[:, k], start=(k == 0), stop=(k == KD - 1))
                        ins.then_inc(logit_done, 1)

                    def gate_up(w, r):
                        for part in range(2):
                            for k in range(KD):
                                ins = nc.tensor.matmul(bank[:, 2 * (r % 2) + part], gate_w(w, part, k), xT[:, k],
                                                       start=(k == 0), stop=(k == KD - 1))
                        ins.then_inc(gu_done, 1)

                    def down(w, i, r, first):
                        pe.wait_ge(hid_ready, i + 1)
                        for t in range(NT):
                            if not first:
                                pe.wait_ge(acc_ready, i * NT + (t + 1 - NT))
                            nc.tensor.matmul(bank[:, 4 + t], hid[:, r % 2, t * P:(t + 1) * P], down_w(w),
                                             start=True, stop=True).then_inc(eo_done, 1)

                    gate_up(wsh_sb, 0)
                    pe.wait_ge(logit_ready, 1)
                    down(wsh_sb, 0, 0, True)
                    with pe.Fori(0, E // RING) as q:
                        for r in range(RING):
                            pe.wait_ge(ld_e[r], q * 16 + 16)
                            gate_up(ring[:, r], r + 1)
                            down(ring[:, r], q * RING + (r + 1), r + 1, False)


def kernel(**inputs):
    import numpy as np
    import concourse.bacc as bacc
    from concourse.bass_utils import run_bass_kernel_spmd

    a = {k: np.asarray(v) for k, v in inputs.items()}
    x = a["x"].reshape(-1, a["x"].shape[-1])
    D = x.shape[1]
    KD = D // P
    ctx = a["ctx_2048"]
    B, L, _ = ctx.shape
    NCH = -(-L // P)
    rows = np.zeros((B, NCH * P, D), ctx.dtype)
    rows[:, :L] = ctx
    rows = rows.reshape(B, NCH, P, D)
    cols = rows.reshape(B, NCH, P, KD, P).transpose(0, 1, 4, 3, 2).reshape(B, NCH, P, KD * P)
    mask = np.zeros((B, NCH * P), np.bool_)
    mask[:, :L] = a["mask_BxS2_bk0"]

    def by_k(w):
        return w.reshape(KD, P, -1).transpose(1, 0, 2)

    def gated(gate_up, down):
        lead = gate_up.shape[:-2]
        g = gate_up.reshape(*lead, 2, P, KD, P)
        n = len(lead)
        g = g.transpose(*range(n), n + 3, n + 2, n, n + 1).reshape(*lead, P, KD * 2 * P)
        return np.concatenate([g, np.swapaxes(down, -1, -2)], axis=-1)

    arrays = {
        "x": x, "ctx_rows": rows, "ctx_cols": cols, "mask": mask,
        "w_qkv": by_k(a["L0_attn_w_qkv"]), "w_out": by_k(a["L0_attn_w_out"]),
        "w_router": by_k(np.concatenate([a["L0_ffn_router_w"], a["L0_ffn_shared_expert_gate_w"]], axis=0).T),
        "w_shared": gated(np.concatenate([a["L0_ffn_shared_gate_w"], a["L0_ffn_shared_up_w"]], axis=0),
                          a["L0_ffn_shared_down_w"]),
        "w_expert": gated(a["L0_ffn_gate_up_proj"], a["L0_ffn_down_proj"]),
    }
    nc = bacc.Bacc("TRN2", target_bir_lowering=False, num_devices=1)
    given, args = {}, []
    for name, arr in arrays.items():
        arr = np.ascontiguousarray(arr)
        given[f"in_{name}"] = arr
        args.append(nc.dram_tensor(f"in_{name}", arr.shape, mybir.dt.from_np(arr.dtype), kind="ExternalInput").ap())
    args.append(nc.dram_tensor("out_y", x.shape, F32, kind="ExternalOutput").ap())
    build_program(nc, *args)
    res = run_bass_kernel_spmd(nc, [given], core_ids=[0])
    return res.results[0]["out_y"].reshape(a["x"].shape)
```

```python
from contextlib import ExitStack

import concourse.bass as bass
from concourse import mybir

ALU = mybir.AluOpType
ACT = mybir.ActivationFunctionType
F32 = mybir.dt.float32
BF16 = mybir.dt.bfloat16
U8 = mybir.dt.uint8
I32 = mybir.dt.int32
AX_X = mybir.AxisListType.X

P = 128
S = 64
HB = P // S
NEG_MASK = 1.0e30
NEG_CAUSAL = 1.0e10
EPS = 1e-5


def build_program(nc, x, ctx_rows, ctx_cols, mask, w_qkv, w_out, w_router, w_shared, w_expert, out, tokens, rows):
    T, D = x.shape
    NT = T // P
    KD = D // P
    B, NCH = ctx_rows.shape[:2]
    M = NCH * P
    HEADS, DH = 16, D // 16
    RG = P // DH
    NG = HEADS // RG
    E = w_expert.shape[0]
    I = P
    SC_CTX = float(D) ** -0.5
    SC_HEAD = float(DH) ** -0.5
    EO = E + 1
    RING = 8
    TOP = 8
    OVER = T * TOP // P - 1
    ITEMS = E + OVER
    NONE = 8192
    NCOL = 6
    GB, EB = 4, 4
    CONSTS = 8
    WE = KD * 2 * I + D
    assert E % RING == 0 and RING % GB == 0 and RING % EB == 0 and TOP * T <= NONE

    with ExitStack() as st:
        def sb(name, shape, dt=F32):
            return st.enter_context(nc.sbuf_tensor(name, shape, dt))

        def sem(name):
            return st.enter_context(nc.semaphore(name))

        bank = st.enter_context(nc.psum_tensor("bank", [P, 8, 512], F32))

        ident = sb("ident", [P, P])
        xt = sb("xt", [P, NT, D])
        xn = sb("xn", [P, NT, D])
        xT = sb("xT", [P, KD, T])
        stats = sb("stats", [P, NT, 6])
        mv = sb("mv", [P, NT, 2])
        var = sb("var", [P, NT])
        std = sb("std", [P, NT])
        rstd = sb("rstd", [P, NT])
        wr_sb = sb("wr_sb", [P, KD, EO])
        wsh_sb = sb("wsh_sb", [P, WE])
        ring = sb("ring", [P, RING, WE])
        ld_e = [sem(f"ld_e{u}") for u in range(RING)]
        tokens_stored = sem("tokens_stored")
        early = ExitStack()
        causal = early.enter_context(nc.sbuf_tensor("causal", [P, HEADS, S], F32))
        wqkv_sb = early.enter_context(nc.sbuf_tensor("wqkv_sb", [P, KD, 3 * D], F32))
        wout_sb = early.enter_context(nc.sbuf_tensor("wout_sb", [P, KD, D], F32))

        def norm_tiles(vec, step, std_ready, xn_ready):
            for j in range(NT):
                nc.vector.bn_stats(stats[:, j], xt[:, j]).then_inc(step, 1)
            vec.wait_ge(step, NT)
            for j in range(NT):
                nc.vector.bn_aggr(mv[:, j], stats[:, j]).then_inc(step, 1)
            vec.wait_ge(step, 2 * NT)
            nc.vector.tensor_scalar(var[:], mv[:, :, 1], EPS, None, ALU.add).then_inc(step, 1)
            vec.wait_ge(std_ready, 1)
            nc.vector.reciprocal(rstd[:], std[:]).then_inc(step, 1)
            vec.wait_ge(step, 2 * NT + 2)
            for j in range(NT):
                nc.vector.tensor_scalar(xn[:, j], xt[:, j], mv[:, j, 0:1], rstd[:, j:j + 1],
                                        ALU.subtract, ALU.mult).then_inc(xn_ready, 1)

        with ExitStack() as ph:
            def sbp(name, shape, dt=F32):
                return ph.enter_context(nc.sbuf_tensor(name, shape, dt))

            def semp(name):
                return ph.enter_context(nc.semaphore(name))

            cT = sbp("cT", [P, NCH, KD * P])
            cR = sbp("cR", [P, NCH, D])
            mrow = sbp("mrow", [P, NT, M], U8)
            bias = sbp("bias", [P, M])
            prob = sbp("prob", [P, M])
            probT = sbp("probT", [P, NCH, P])
            rmax = sbp("rmax", [P, NT])
            nmax = sbp("nmax", [P, NT])
            rsum = sbp("rsum", [P, NT])
            rinv = sbp("rinv", [P, NT])
            anyv = sbp("anyv", [P, NT])
            gain = sbp("gain", [P, NT])

            ld_x, ld_mask = semp("ld_x"), semp("ld_mask")
            ld_w = sem("ld_w")
            ld_cT = [semp(f"ld_cT{c}") for c in range(NCH)]
            ld_cR = [semp(f"ld_cR{c}") for c in range(NCH)]
            ident_ready, ident_zero = semp("ident_ready"), semp("ident_zero")
            causal_zero, causal_ready = semp("causal_zero"), semp("causal_ready")
            ln_step = semp("ln_step")
            std_ready = semp("std_ready")
            xn_ready = semp("xn_ready")
            xT_done, xT_ready = semp("xT_done"), semp("xT_ready")
            scores_done = semp("scores_done")
            bias_ready = semp("bias_ready")
            anyv_ready = semp("anyv_ready")
            scores_read = semp("scores_read")
            max_ready, nmax_ready = semp("max_ready"), semp("nmax_ready")
            exp_ready = semp("exp_ready")
            pT_done, pT_copied = semp("pT_done"), semp("pT_copied")
            pv_done = semp("pv_done")
            rinv_ready, gain_ready = semp("rinv_ready"), semp("gain_ready")
            x1_ready = semp("x1_ready")
            NPT = -(-NCH // 4)

            with nc.Block() as block:
                @block.sync
                def _(sp):
                    sp.dma_start(xt[:], x.rearrange("(t p) d -> p t d", p=P)).then_inc(ld_x, 16)
                    for half in range(HB):
                        sp.dma_start(mrow[half * S:(half + 1) * S],
                                     mask.rearrange("(j h) m -> h j m", h=HB)[half].partition_broadcast(S)
                                     ).then_inc(ld_mask, 16)
                    for b in range(B):
                        for c in range(NCH):
                            if b:
                                sp.wait_ge(scores_done, NCH * (b - 1) + c + 1)
                            sp.dma_start(cT[:, c], ctx_cols[b, c]).then_inc(ld_cT[c], 16)

                @block.gpsimd
                def _(pool):
                    nc.gpsimd.memset(ident[:], 0.0).then_inc(ident_zero, 1)
                    pool.wait_ge(ident_zero, 1)
                    nc.gpsimd.affine_select(out=ident[:], in_=ident[:], compare_op=ALU.not_equal, fill=1.0,
                                            base=0, pattern=[[-1, P]], channel_multiplier=1).then_inc(ident_ready, 1)
                    for half in range(HB):
                        nc.gpsimd.memset(causal[half * S:(half + 1) * S], 0.0).then_inc(causal_zero, 1)
                        pool.wait_ge(causal_zero, half + 1)
                        nc.gpsimd.affine_select(out=causal[half * S:(half + 1) * S],
                                                in_=causal[half * S:(half + 1) * S],
                                                compare_op=ALU.is_ge, fill=-NEG_CAUSAL, base=0,
                                                pattern=[[0, HEADS], [-1, S]],
                                                channel_multiplier=1).then_inc(causal_ready, 1)
                    pool.wait_ge(causal_ready, HB)
                    pool.wait_ge(ld_mask, 16 * HB)
                    for j in range(NT):
                        if j:
                            pool.wait_ge(scores_read, j)
                        nc.gpsimd.tensor_scalar(bias[:], mrow[:, j], -1.0, NEG_MASK,
                                                ALU.add, ALU.mult).then_inc(bias_ready, 1)

                @block.scalar
                def _(act):
                    act.dma_start(wqkv_sb[:], w_qkv).then_inc(ld_w, 16)
                    act.dma_start(wout_sb[:], w_out).then_inc(ld_w, 16)
                    act.dma_start(wr_sb[:], w_router).then_inc(ld_w, 16)
                    act.dma_start(wsh_sb[:], w_shared).then_inc(ld_w, 16)
                    act.wait_ge(ln_step, 2 * NT + 1)
                    nc.scalar.activation(std[:], var[:], ACT.Sqrt).then_inc(std_ready, 1)

                    def load_rows(b):
                        for c in range(NCH):
                            if b:
                                act.wait_ge(pv_done, NCH * (b - 1) + c + 1)
                            act.dma_start(cR[:, c], ctx_rows[b, c]).then_inc(ld_cR[c], 16)

                    load_rows(0)
                    for j in range(NT):
                        act.wait_ge(xT_done, j + 1)
                        nc.scalar.activation(xT[:, :, j * P:(j + 1) * P],
                                             bank[:, 6 + j % 2].rearrange("p (k t) -> p k t", k=KD),
                                             ACT.Copy).then_inc(xT_ready, 1)
                    for j in range(NT):
                        act.wait_ge(nmax_ready, j + 1)
                        nc.scalar.activation(prob[:], prob[:], ACT.Exp, bias=nmax[:, j:j + 1],
                                             accum_out=rsum[:, j:j + 1]).then_inc(exp_ready, 1)
                        for g in range(NPT):
                            act.wait_ge(pT_done, NPT * j + g + 1)
                            n = min(4, NCH - 4 * g)
                            nc.scalar.activation(probT[:, 4 * g:4 * g + n],
                                                 bank[:, 4 + g % 2, 0:n * P].rearrange("p (c q) -> p c q", c=n),
                                                 ACT.Copy).then_inc(pT_copied, 1)
                        load_rows(HB * j + 1)
                        if j + 1 < NT:
                            load_rows(HB * j + 2)

                @block.vector
                def _(vec):
                    vec.wait_ge(ld_x, 16)
                    norm_tiles(vec, ln_step, std_ready, xn_ready)
                    vec.wait_ge(ld_mask, 16 * HB)
                    nc.vector.tensor_reduce(anyv[:], mrow[:], AX_X, ALU.max).then_inc(anyv_ready, 1)
                    vec.wait_ge(anyv_ready, 1)
                    for j in range(NT):
                        vec.wait_ge(scores_done, NCH * HB * (j + 1))
                        vec.wait_ge(bias_ready, j + 1)
                        if j:
                            vec.wait_ge(pT_done, NPT * j)
                        nc.vector.scalar_tensor_tensor(
                            out=prob[:], in0=bank[:, 0:4].rearrange("p b n -> p (b n)")[:, 0:M],
                            scalar=SC_CTX, in1=bias[:], op0=ALU.mult, op1=ALU.add).then_inc(scores_read, 1)
                        vec.wait_ge(scores_read, j + 1)
                        nc.vector.tensor_reduce(rmax[:, j:j + 1], prob[:], AX_X, ALU.max).then_inc(max_ready, 1)
                        vec.wait_ge(max_ready, j + 1)
                        nc.vector.tensor_scalar(nmax[:, j:j + 1], rmax[:, j:j + 1], -1.0, None,
                                                ALU.mult).then_inc(nmax_ready, 1)
                        vec.wait_ge(exp_ready, j + 1)
                        nc.vector.reciprocal(rinv[:, j:j + 1], rsum[:, j:j + 1]).then_inc(rinv_ready, 1)
                        vec.wait_ge(rinv_ready, j + 1)
                        nc.vector.tensor_tensor(gain[:, j:j + 1], rinv[:, j:j + 1], anyv[:, j:j + 1],
                                                ALU.mult).then_inc(gain_ready, 1)
                        vec.wait_ge(gain_ready, j + 1)
                        vec.wait_ge(pv_done, NCH * HB * (j + 1))
                        nc.vector.scalar_tensor_tensor(out=xt[:, j], in0=bank[:, 6 + j % 2], scalar=gain[:, j:j + 1],
                                                       in1=xt[:, j], op0=ALU.mult, op1=ALU.add).then_inc(x1_ready, 1)

                @block.tensor
                def _(pe):
                    pe.wait_ge(ident_ready, 1)
                    for j in range(NT):
                        pe.wait_ge(xn_ready, j + 1)
                        if j >= 2:
                            pe.wait_ge(xT_ready, j - 1)
                        for k in range(KD):
                            ins = nc.tensor.transpose(bank[:, 6 + j % 2, k * P:(k + 1) * P],
                                                      xn[:, j, k * P:(k + 1) * P], ident[:])
                        ins.then_inc(xT_done, 1)
                    pe.wait_ge(xT_ready, NT)

                    def scores(j):
                        if j:
                            pe.wait_ge(scores_read, j)
                        for half in range(HB):
                            b = HB * j + half
                            tok = slice(b * S, (b + 1) * S)
                            for c in range(NCH):
                                pe.wait_ge(ld_cT[c], 16 * (b + 1))
                                for k in range(KD):
                                    ins = nc.tensor.matmul(
                                        bank[half * S:(half + 1) * S, c // 4, (c % 4) * P:(c % 4 + 1) * P],
                                        xT[:, k, tok], cT[:, c, k * P:(k + 1) * P],
                                        start=(k == 0), stop=(k == KD - 1))
                                ins.then_inc(scores_done, 1)

                    def attend(j):
                        pe.wait_ge(exp_ready, j + 1)
                        for g in range(NPT):
                            if NPT * j + g >= 2:
                                pe.wait_ge(pT_copied, NPT * j + g - 1)
                            for c in range(4 * g, min(4 * g + 4, NCH)):
                                ins = nc.tensor.transpose(bank[:, 4 + g % 2, (c % 4) * P:(c % 4 + 1) * P],
                                                          prob[:, c * P:(c + 1) * P], ident[:])
                            ins.then_inc(pT_done, 1)
                        if j >= 2:
                            pe.wait_ge(x1_ready, j - 1)
                        for half in range(HB):
                            b = HB * j + half
                            for c in range(NCH):
                                if half == 0:
                                    pe.wait_ge(pT_copied, NPT * j + c // 4 + 1)
                                pe.wait_ge(ld_cR[c], 16 * (b + 1))
                                nc.tensor.matmul(bank[half * S:(half + 1) * S, 6 + j % 2],
                                                 probT[:, c, half * S:(half + 1) * S], cR[:, c],
                                                 start=(c == 0), stop=(c == NCH - 1)).then_inc(pv_done, 1)

                    scores(0)
                    for j in range(NT):
                        if j + 1 < NT:
                            scores(j + 1)
                        attend(j)

        with ExitStack() as ph:
            def sbp(name, shape, dt=F32):
                return ph.enter_context(nc.sbuf_tensor(name, shape, dt))

            def semp(name):
                return ph.enter_context(nc.semaphore(name))

            qkT = sbp("qkT", [P, 2 * NG, T])
            v = sbp("v", [P, NT, D])
            vswap = sbp("vswap", [P, NT, D])
            sc = sbp("sc", [P, 2, HEADS, S])
            pT = sbp("pT", [P, 2, HEADS // 2, P])
            o = sbp("o", [P, NT, D])
            oT = sbp("oT", [P, KD, T])
            hmax = sbp("hmax", [P, NT, HEADS])
            hsum = sbp("hsum", [P, NT, HEADS])
            hinv = sbp("hinv", [P, NT, HEADS])

            b_ln, b_std, b_xn = semp("b_ln"), semp("b_std"), semp("b_xn")
            b_xT_done, b_xT_ready = semp("b_xT_done"), semp("b_xT_ready")
            qk_done, qk_ready = semp("qk_done"), semp("qk_ready")
            v_done, v_ready, vswap_ready = semp("v_done"), semp("v_ready"), semp("vswap_ready")
            hs_done, hs_read = semp("hs_done"), semp("hs_read")
            hmax_ready, sub_ready, hexp_ready = semp("hmax_ready"), semp("sub_ready"), semp("hexp_ready")
            hsum_ready, hinv_ready = semp("hsum_ready"), semp("hinv_ready")
            hpT_done, hpT_copied = semp("hpT_done"), semp("hpT_copied")
            ho_done, o_ready = semp("ho_done"), semp("o_ready")
            oT_done, oT_ready = semp("oT_done"), semp("oT_ready")
            y_done, x2_ready = semp("y_done"), semp("x2_ready")

            with nc.Block() as block:
                @block.sync
                def _(sp):
                    for u in range(RING):
                        sp.dma_start(ring[:, u], w_expert[u]).then_inc(ld_e[u], 16)
                    for half in range(HB):
                        sp.wait_ge(v_ready, NT)
                        lo, hi = half * S, (1 - half) * S
                        sp.dma_start(vswap[lo:lo + S], v[hi:hi + S]).then_inc(vswap_ready, 16)

                @block.vector
                def _(vec):
                    norm_tiles(vec, b_ln, b_std, b_xn)
                    for t in range(NT):
                        vec.wait_ge(v_done, t + 1)
                        nc.vector.tensor_copy(v[:, t], bank[:, 4 + t]).then_inc(v_ready, 1)

                    def softmax(j):
                        buf = sc[:, j % 2]
                        vec.wait_ge(hs_done, j + 1)
                        if j >= 2:
                            vec.wait_ge(hpT_done, 2 * (j - 1))
                        nc.vector.scalar_tensor_tensor(
                            out=buf.rearrange("p (r g) k -> p r g k", r=RG),
                            in0=bank[:, 0:4, 0:NG * S].rearrange("p r (g k) -> p r g k", g=NG), scalar=SC_HEAD,
                            in1=causal[:].rearrange("p (r g) k -> p r g k", r=RG), op0=ALU.mult, op1=ALU.add).then_inc(hs_read, 1)
                        vec.wait_ge(hs_read, j + 1)
                        nc.vector.tensor_reduce(hmax[:, j], buf, AX_X, ALU.max).then_inc(hmax_ready, 1)
                        vec.wait_ge(hmax_ready, j + 1)
                        nc.vector.tensor_tensor(buf, buf, hmax[:, j].unsqueeze(2).broadcast_to([P, HEADS, S]),
                                                ALU.subtract).then_inc(sub_ready, 1)

                    def finish(j):
                        vec.wait_ge(hexp_ready, j + 1)
                        nc.vector.tensor_reduce(hsum[:, j], sc[:, j % 2], AX_X, ALU.add).then_inc(hsum_ready, 1)
                        vec.wait_ge(hsum_ready, j + 1)
                        nc.vector.reciprocal(hinv[:, j], hsum[:, j]).then_inc(hinv_ready, 1)
                        vec.wait_ge(hinv_ready, j + 1)
                        vec.wait_ge(ho_done, j + 1)
                        for hh in range(2):
                            ov = o[:, j].rearrange("p (gp hh r d) -> p hh r gp d", gp=NG // 2, hh=2, r=RG)[:, hh]
                            iv = hinv[:, j].rearrange("p (r gp hh) -> p hh r gp", r=RG, hh=2)[:, hh]
                            nc.vector.tensor_tensor(
                                ov, bank[:, 6 + hh, 0:HEADS // 2 * DH].rearrange("p (r gp d) -> p r gp d", r=RG, gp=NG // 2),
                                iv.unsqueeze(3).broadcast_to([P, RG, NG // 2, DH]), ALU.mult).then_inc(o_ready, 1)

                    softmax(0)
                    for j in range(NT):
                        if j + 1 < NT:
                            softmax(j + 1)
                        finish(j)
                    for j in range(NT):
                        vec.wait_ge(y_done, j + 1)
                        nc.vector.tensor_tensor(xt[:, j], bank[:, 4 + j], xt[:, j], ALU.add).then_inc(x2_ready, 1)

                @block.scalar
                def _(act):
                    act.wait_ge(b_ln, 2 * NT + 1)
                    nc.scalar.activation(std[:], var[:], ACT.Sqrt).then_inc(b_std, 1)
                    for j in range(NT):
                        act.wait_ge(b_xT_done, j + 1)
                        nc.scalar.activation(xT[:, :, j * P:(j + 1) * P],
                                             bank[:, j].rearrange("p (k t) -> p k t", k=KD),
                                             ACT.Copy).then_inc(b_xT_ready, 1)
                    for g in range(2 * NG):
                        act.wait_ge(qk_done, g + 1)
                        nc.scalar.activation(qkT[:, g], bank[:, g % 4], ACT.Copy).then_inc(qk_ready, 1)

                    def copies(j):
                        for n in range(2):
                            act.wait_ge(hpT_done, 2 * j + n + 1)
                            if j >= 2:
                                act.wait_ge(ho_done, j - 1)
                            nc.scalar.activation(pT[:, j % 2, 4 * n:4 * n + 4],
                                                 bank[:, 4 + n].rearrange("p (c q) -> p c q", c=4),
                                                 ACT.Copy).then_inc(hpT_copied, 1)

                    for j in range(NT):
                        act.wait_ge(sub_ready, j + 1)
                        nc.scalar.activation(sc[:, j % 2], sc[:, j % 2], ACT.Exp).then_inc(hexp_ready, 1)
                        if j:
                            copies(j - 1)
                    copies(NT - 1)
                    for j in range(NT):
                        act.wait_ge(oT_done, j + 1)
                        nc.scalar.activation(oT[:, :, j * P:(j + 1) * P],
                                             bank[:, j].rearrange("p (k t) -> p k t", k=KD),
                                             ACT.Copy).then_inc(oT_ready, 1)

                @block.tensor
                def _(pe):
                    for j in range(NT):
                        pe.wait_ge(b_xn, j + 1)
                        for k in range(KD):
                            ins = nc.tensor.transpose(bank[:, j, k * P:(k + 1) * P],
                                                      xn[:, j, k * P:(k + 1) * P], ident[:])
                        ins.then_inc(b_xT_done, 1)
                    pe.wait_ge(ld_w, 16 * 4)
                    for t in range(NT):
                        pe.wait_ge(b_xT_ready, t + 1)
                        for k in range(KD):
                            ins = nc.tensor.matmul(bank[:, 4 + t], xT[:, k, t * P:(t + 1) * P],
                                                   wqkv_sb[:, k, 2 * D:3 * D], start=(k == 0), stop=(k == KD - 1))
                        ins.then_inc(v_done, 1)
                    for g in range(2 * NG):
                        if g >= 4:
                            pe.wait_ge(qk_ready, g - 3)
                        for k in range(KD):
                            ins = nc.tensor.matmul(bank[:, g % 4], wqkv_sb[:, k, g * P:(g + 1) * P], xT[:, k],
                                                   start=(k == 0), stop=(k == KD - 1))
                        ins.then_inc(qk_done, 1)

                    def scores(j):
                        if j == 0:
                            pe.wait_ge(qk_ready, 2 * NG)
                        else:
                            pe.wait_ge(hs_read, j)
                        for g in range(NG):
                            for r in range(RG):
                                rows = slice(r * DH, (r + 1) * DH)
                                for half in range(HB):
                                    tok = slice((HB * j + half) * S, (HB * j + half + 1) * S)
                                    ins = nc.tensor.matmul(bank[half * S:(half + 1) * S, r, g * S:(g + 1) * S],
                                                           qkT[rows, g, tok], qkT[rows, NG + g, tok],
                                                           start=True, stop=True, tile_position=(r * DH, half * S))
                        ins.then_inc(hs_done, 1)

                    def attend(j):
                        pe.wait_ge(hexp_ready, j + 1)
                        for n in range(2):
                            if j == 0:
                                pe.wait_ge(v_ready, NT)
                            else:
                                pe.wait_ge(hpT_copied, 2 * (j - 1) + n + 1)
                            for c in range(4):
                                tp = 4 * n + c
                                ins = nc.tensor.transpose(
                                    bank[:, 4 + n, c * P:(c + 1) * P],
                                    sc[:, j % 2, 2 * tp:2 * tp + 2].rearrange("p h k -> p (h k)"), ident[:])
                            ins.then_inc(hpT_done, 1)
                        pe.wait_ge(vswap_ready, 16 * HB)
                        if j:
                            pe.wait_ge(o_ready, 2 * j)
                        for n in range(2):
                            pe.wait_ge(hpT_copied, 2 * j + n + 1)
                            for c in range(4):
                                tp = 4 * n + c
                                r, gp = tp // (NG // 2), tp % (NG // 2)
                                for hh in range(2):
                                    h = RG * (2 * gp + hh) + r
                                    for half in range(HB):
                                        vv = v if half == hh else vswap
                                        ins = nc.tensor.matmul(
                                            bank[half * S:(half + 1) * S, 6 + hh, tp * DH:(tp + 1) * DH],
                                            pT[hh * S:(hh + 1) * S, j % 2, tp, half * S:(half + 1) * S],
                                            vv[hh * S:(hh + 1) * S, j, h * DH:(h + 1) * DH],
                                            start=True, stop=True, tile_position=(hh * S, half * S))
                        ins.then_inc(ho_done, 1)

                    scores(0)
                    for j in range(NT):
                        if j + 1 < NT:
                            scores(j + 1)
                        attend(j)
                    pe.wait_ge(hs_read, NT)
                    for j in range(NT):
                        pe.wait_ge(o_ready, 2 * (j + 1))
                        for k in range(KD):
                            ins = nc.tensor.transpose(bank[:, j, k * P:(k + 1) * P],
                                                      o[:, j, k * P:(k + 1) * P], ident[:])
                        ins.then_inc(oT_done, 1)
                    for j in range(NT):
                        pe.wait_ge(oT_ready, j + 1)
                        for k in range(KD):
                            ins = nc.tensor.matmul(bank[:, 4 + j], oT[:, k, j * P:(j + 1) * P], wout_sb[:, k],
                                                   start=(k == 0), stop=(k == KD - 1))
                        ins.then_inc(y_done, 1)

        early.close()
        gpos = sb("gpos", [P, NT, E])
        jtab = sb("jtab", [P, ITEMS])
        slot_no = sb("slot_no", [P, P], BF16)
        gathered = sb("gathered", [P, GB, D])
        info = sb("info", [P, NT, E, NCOL], BF16)
        sgate = sb("sgate", [P, NT])
        over_e = sb("over_e", [1, OVER], I32)
        over_n = sb("over_n", [1, 1], I32)
        with ExitStack() as ph:
            def sbp(name, shape, dt=F32):
                return ph.enter_context(nc.sbuf_tensor(name, shape, dt))

            def semp(name):
                return ph.enter_context(nc.semaphore(name))

            logit = sbp("logit", [P, NT, EO])
            top8 = sbp("top8", [P, NT, 8])
            rest = sbp("rest", [P, NT, E])
            chosen = sbp("chosen", [P, NT, E])
            chosen_b = sbp("chosen_b", [P, NT, E], BF16)
            chosenT = sbp("chosenT", [E, NT, P], BF16)
            lexp = sbp("lexp", [P, NT, E])
            nl = sbp("nl", [P, NT])
            wsum = sbp("wsum", [P, NT])
            winv = sbp("winv", [P, NT])
            comb = sbp("comb", [P, NT, E])
            left = sbp("left", [P, 2, NT, E])
            pos = sbp("pos", [P, NT, E])
            g1 = sbp("g1", [P, NT, E])
            g2 = sbp("g2", [P, NT, E])
            rank = sbp("rank", [P, NT, E])
            tri = sbp("tri", [P, P], BF16)
            ones = sbp("ones", [P, P], BF16)
            ident_b = sbp("ident_b", [P, P], BF16)
            ci = sbp("ci", [P, ITEMS], I32)
            cp = sbp("cp", [P, 1], I32)
            cpf = sbp("cpf", [P, 1])
            ce = sbp("ce", [P, E])
            cover = sbp("cover", [P, E])
            ctile = sbp("ctile", [P, NT])
            cnt = sbp("cnt", [E, 1])
            ovc = sbp("ovc", [E, 4])
            ovb = sbp("ovb", [E, P], BF16)
            cum = sbp("cum", [P, E + 1])
            shift = sbp("shift", [P, E])
            below = sbp("below", [1, OVER, E])
            over_f = sbp("over_f", [1, OVER + 1])

            c_ln, c_std, c_xn = semp("c_ln"), semp("c_std"), semp("c_xn")
            c_xT_done, c_xT_ready = semp("c_xT_done"), semp("c_xT_ready")
            logit_done, logit_ready = semp("logit_done"), semp("logit_ready")
            step, lexp_ready, chosen_ready = semp("step"), semp("lexp_ready"), semp("chosen_ready")
            const, cast = semp("const"), semp("cast")
            count_done, ovb_ready, cum_done = semp("count_done"), semp("ovb_ready"), semp("cum_done")
            pos_done, chT_done, chT_ready, rank_done = semp("pos_done"), semp("chT_done"), semp("chT_ready"), semp("rank_done")

            with nc.Block() as block:
                @block.sync
                def _(sp):
                    sp.wait_ge(c_xn, NT)
                    sp.dma_start(tokens.rearrange("(t p) d -> p t d", p=P), xn[:]).then_inc(tokens_stored, 16)

                @block.gpsimd
                def _(pool):
                    n = 0
                    for t, pattern, base, mult in ((ci[:], [[P, ITEMS]], 0, 0), (cp[:], [[0, 1]], 0, 1)):
                        nc.gpsimd.iota(t, pattern=pattern, base=base, channel_multiplier=mult).then_inc(const, 1)
                        n += 1
                    for t, v in ((tri, 1.0), (ones, 1.0), (ident_b, 0.0)):
                        nc.gpsimd.memset(t[:], v).then_inc(const, 1)
                        n += 1
                    pool.wait_ge(const, n)
                    nc.gpsimd.affine_select(out=tri[:], in_=tri[:], compare_op=ALU.is_gt, fill=0.0, base=0,
                                            pattern=[[1, P]], channel_multiplier=-1).then_inc(const, 1)
                    nc.gpsimd.affine_select(out=ident_b[:], in_=ident_b[:], compare_op=ALU.not_equal, fill=1.0,
                                            base=0, pattern=[[-1, P]], channel_multiplier=1).then_inc(const, 1)
                    n += 2
                    pool.wait_ge(const, n)
                    nc.gpsimd.memset(gathered[:], 0.0).then_inc(const, 1)
                    assert n + 1 == CONSTS

                @block.vector
                def _(vec):
                    norm_tiles(vec, c_ln, c_std, c_xn)
                    vec.wait_ge(const, CONSTS)
                    nc.vector.tensor_copy(jtab[:], ci[:]).then_inc(cast, 1)
                    nc.vector.tensor_copy(cpf[:], cp[:]).then_inc(cast, 1)
                    vec.wait_ge(cast, 2)
                    nc.vector.tensor_scalar(slot_no[:, 0:ITEMS], jtab[:], 1.0 / P, None, ALU.mult).then_inc(cast, 1)
                    nc.vector.tensor_scalar(slot_no[:, ITEMS:P], jtab[:, 0:P - ITEMS], 1.0 / P, float(ITEMS),
                                            ALU.mult, ALU.add).then_inc(cast, 1)
                    nc.vector.tensor_scalar(ce[:], jtab[:, 0:E], 1.0, None, ALU.add).then_inc(cast, 1)
                    nc.vector.tensor_scalar(cover[:], jtab[:, 0:E], -1.0, float(P * (E - 1)),
                                            ALU.mult, ALU.add).then_inc(cast, 1)
                    nc.vector.tensor_scalar(ctile[:], jtab[:, 0:NT], -float(NONE), None, ALU.add).then_inc(cast, 1)
                    vec.wait_ge(logit_done, NT)
                    nc.vector.tensor_copy(logit[:], bank[:, 6, 0:NT * EO].rearrange("p (t e) -> p t e", t=NT)
                                          ).then_inc(logit_ready, 1)
                    vec.wait_ge(logit_ready, 1)
                    for j in range(NT):
                        nc.vector.max(top8[:, j], logit[:, j, 0:E]).then_inc(step, 1)
                    vec.wait_ge(step, NT)
                    nc.vector.tensor_scalar(nl[:], top8[:, :, 0], -1.0, None, ALU.mult).then_inc(step, 1)
                    for j in range(NT):
                        nc.vector.match_replace(rest[:, j], top8[:, j], logit[:, j, 0:E], -3.0e38).then_inc(step, 1)
                    n = [2 * NT + 1]

                    def chain(ins):
                        n[0] += 1
                        ins.then_inc(step, 1)
                        vec.wait_ge(step, n[0])

                    vec.wait_ge(step, n[0])
                    nc.vector.tensor_tensor(chosen_b[:], rest[:], logit[:, :, 0:E], ALU.not_equal
                                            ).then_inc(chosen_ready, 1)
                    nc.vector.tensor_tensor(chosen[:], rest[:], logit[:, :, 0:E], ALU.not_equal
                                            ).then_inc(chosen_ready, 1)
                    vec.wait_ge(chosen_ready, 2)
                    vec.wait_ge(lexp_ready, NT)
                    chain(nc.vector.tensor_tensor(lexp[:], chosen[:], lexp[:], ALU.mult))
                    chain(nc.vector.tensor_reduce(wsum[:], lexp[:], AX_X, ALU.add))
                    chain(nc.vector.reciprocal(winv[:], wsum[:]))
                    chain(nc.vector.tensor_tensor(comb[:], lexp[:], winv[:].unsqueeze(2).broadcast_to([P, NT, E]),
                                                  ALU.mult))
                    chain(nc.vector.tensor_copy(info[:, :, :, 3], comb[:]))
                    chain(nc.vector.tensor_tensor(left[:, 0], comb[:], info[:, :, :, 3], ALU.subtract))
                    chain(nc.vector.tensor_copy(info[:, :, :, 4], left[:, 0]))
                    chain(nc.vector.tensor_tensor(left[:, 1], left[:, 0], info[:, :, :, 4], ALU.subtract))
                    nc.vector.tensor_copy(info[:, :, :, 5], left[:, 1]).then_inc(cast, 1)
                    for t in range(NT):
                        nc.vector.tensor_scalar(info[:, t, :, 0], chosen[:, t], 0.0, cpf[:, 0:1],
                                                ALU.mult, ALU.add).then_inc(cast, 1)
                        nc.vector.tensor_scalar(info[:, t, :, 1], chosen[:, t], 0.0, ctile[:, t:t + 1],
                                                ALU.mult, ALU.add).then_inc(cast, 1)
                    vec.wait_ge(count_done, 1)
                    chain(nc.vector.tensor_copy(cnt[:], bank[0:E, 4, 0:1]))
                    for c in range(1, NT):
                        chain(nc.vector.tensor_scalar(ovc[:, c:c + 1], cnt[:], float(c * P), None, ALU.is_gt))
                    chain(nc.vector.tensor_reduce(ovc[:, 0:1], ovc[:, 1:NT], AX_X, ALU.add))
                    nc.vector.tensor_copy(ovb[:], ovc[:, 0:1].broadcast_to([E, P])).then_inc(ovb_ready, 1)
                    vec.wait_ge(chT_done, 1)
                    nc.vector.tensor_copy(chosenT[:], bank[0:E, 3].rearrange("e (t p) -> e t p", t=NT)
                                          ).then_inc(chT_ready, 1)
                    vec.wait_ge(cum_done, 1)
                    chain(nc.vector.tensor_copy(cum[:], bank[:, 5, 0:E + 1]))
                    vec.wait_ge(pos_done, 1)
                    chain(nc.vector.tensor_copy(pos[:], bank[:, 2, 0:NT * E].rearrange("p (t e) -> p t e", t=NT)))
                    chain(nc.vector.scalar_tensor_tensor(out=shift[:], in0=cum[:, 0:E], scalar=float(P), in1=cover[:],
                                                         op0=ALU.mult, op1=ALU.add))
                    chain(nc.vector.scalar_tensor_tensor(out=g1[:], in0=pos[:], scalar=float(P),
                                                         in1=shift[:].unsqueeze(1).broadcast_to([P, NT, E]),
                                                         op0=ALU.is_ge, op1=ALU.mult))
                    chain(nc.vector.tensor_tensor(g2[:], pos[:], ce[:].unsqueeze(1).broadcast_to([P, NT, E]), ALU.add))
                    chain(nc.vector.tensor_tensor(g1[:], g1[:], g2[:], ALU.add))
                    chain(nc.vector.tensor_tensor(g2[:], g1[:], chosen[:], ALU.mult))
                    chain(nc.vector.tensor_scalar(gpos[:], g2[:], -1.0, None, ALU.add))
                    chain(nc.vector.tensor_tensor(below[:], cum[0:1, 1:E + 1].unsqueeze(1).broadcast_to([1, OVER, E]),
                                                  slot_no[0:1, 0:OVER].unsqueeze(2).broadcast_to([1, OVER, E]), ALU.is_le))
                    chain(nc.vector.tensor_reduce(over_f[:, 0:OVER], below[:], AX_X, ALU.add))
                    nc.vector.tensor_scalar(over_e[:], over_f[:, 0:OVER], float(E - 1), None, ALU.min).then_inc(cast, 1)
                    nc.vector.tensor_scalar(over_n[:], cum[0:1, E:E + 1], 1.0, None, ALU.max).then_inc(cast, 1)
                    vec.wait_ge(rank_done, 1)
                    for t in range(NT):
                        nc.vector.tensor_scalar(info[:, t, :, 2], bank[:, 1, t * E:(t + 1) * E], float(T), ctile[:, t:t + 1],
                                                ALU.mult, ALU.add).then_inc(cast, 1)

                @block.scalar
                def _(act):
                    act.wait_ge(c_ln, 2 * NT + 1)
                    nc.scalar.activation(std[:], var[:], ACT.Sqrt).then_inc(c_std, 1)
                    for j in range(NT):
                        act.wait_ge(c_xT_done, j + 1)
                        nc.scalar.activation(xT[:, :, j * P:(j + 1) * P],
                                             bank[:, j].rearrange("p (k t) -> p k t", k=KD),
                                             ACT.Copy).then_inc(c_xT_ready, 1)
                    act.wait_ge(step, NT + 1)
                    for j in range(NT):
                        nc.scalar.activation(lexp[:, j], logit[:, j, 0:E], ACT.Exp,
                                             bias=nl[:, j:j + 1]).then_inc(lexp_ready, 1)
                    nc.scalar.activation(sgate[:], logit[:, :, E], ACT.Sigmoid).then_inc(cast, 1)

                @block.tensor
                def _(pe):
                    for j in range(NT):
                        pe.wait_ge(c_xn, j + 1)
                        for k in range(KD):
                            ins = nc.tensor.transpose(bank[:, j, k * P:(k + 1) * P],
                                                      xn[:, j, k * P:(k + 1) * P], ident[:])
                        ins.then_inc(c_xT_done, 1)
                    for j in range(NT):
                        pe.wait_ge(c_xT_ready, j + 1)
                        for k in range(KD):
                            ins = nc.tensor.matmul(bank[:, 6, j * EO:(j + 1) * EO], xT[:, k, j * P:(j + 1) * P],
                                                   wr_sb[:, k], start=(k == 0), stop=(k == KD - 1))
                        ins.then_inc(logit_done, 1)
                    pe.wait_ge(chosen_ready, 1)
                    pe.wait_ge(const, CONSTS)
                    for t in range(NT):
                        ins = nc.tensor.matmul(bank[0:E, 4, 0:1], chosen_b[:, t], ones[:, 0:1],
                                               start=(t == 0), stop=(t == NT - 1))
                    ins.then_inc(count_done, 1)
                    for t in range(NT):
                        ins = nc.tensor.matmul(bank[0:E, 3, t * P:(t + 1) * P], chosen_b[:, t], ident_b[:],
                                               start=True, stop=True)
                    ins.then_inc(chT_done, 1)
                    for t in range(NT):
                        for u in range(t + 1):
                            ins = nc.tensor.matmul(bank[:, 2, t * E:(t + 1) * E], (tri if u == t else ones)[:],
                                                   chosen_b[:, u], start=(u == 0), stop=(u == t))
                    ins.then_inc(pos_done, 1)
                    pe.wait_ge(ovb_ready, 1)
                    nc.tensor.matmul(bank[:, 5, 0:E + 1], ovb[:], tri[0:E, 0:E + 1], start=True, stop=True
                                     ).then_inc(cum_done, 1)
                    pe.wait_ge(chT_ready, 1)
                    for t in range(NT):
                        ins = nc.tensor.matmul(bank[:, 1, t * E:(t + 1) * E], chosenT[:, t], tri[0:E, 0:E],
                                               start=True, stop=True)
                    ins.then_inc(rank_done, 1)

        with ExitStack() as ph:
            def sbp(name, shape, dt=F32):
                return ph.enter_context(nc.sbuf_tensor(name, shape, dt))

            def semp(name):
                return ph.enter_context(nc.semaphore(name))

            pick = sbp("pick", [P, 2, NT, P], BF16)
            idx = sbp("idx", [P, RING, 2], I32)
            wslot = sbp("wslot", [P, RING])
            slotT = sbp("slotT", [P, 2, KD, P])
            sil = sbp("sil", [P, 2, P])
            hid = sbp("hid", [P, 2, P])
            eo = sbp("eo", [P, RING // 2, D])
            part = sbp("part", [P, NT, TOP, D])
            ssil = sbp("ssil", [P, T])
            shid = sbp("shid", [P, T])
            total = sbp("total", [P, NT, D])

            picked = semp("picked")
            idx_done, idx_ready = semp("idx_done"), semp("idx_ready")
            ld_g = [semp(f"ld_g{u}") for u in range(GB)]
            sT_done, sT_ready = semp("sT_done"), semp("sT_ready")
            gu_done, sil_ready, hid_ready = semp("gu_done"), semp("sil_ready"), semp("hid_ready")
            eo_done, eo_ready = semp("eo_done"), semp("eo_ready")
            st_e = [semp(f"st_e{u}") for u in range(RING // 2)]

            pool_steps = semp("pool_steps")

            def item(q, m):
                return q * RING + m

            def fours(q, m):
                return q * (RING // 4) + m // 4

            def at_least(eng, s, v):
                if not isinstance(v, int) or v > 0:
                    eng.wait_ge(s, v)

            def exists(q, m):
                return not isinstance(q, int) or 0 <= item(q, m) < E

            def gate_w(w, half, k):
                return w[:, (k * 2 + half) * I:(k * 2 + half + 1) * I]

            def down_w(w):
                return w[:, KD * 2 * I:WE]

            def column(q, m):
                return bass.ds(item(q, m), 1) if not isinstance(q, int) else slice(item(q, m), item(q, m) + 1)

            def pick_slots(b, jcol, col):
                for t in range(NT):
                    ins = nc.vector.tensor_scalar(pick[:, b, t], slot_no[:], jcol, gpos[:, t, col],
                                                  ALU.add, ALU.is_equal)
                return ins

            def index_products(b, col):
                for t in range(NT):
                    ins = nc.tensor.matmul(bank[:, 7, 0:NCOL], pick[:, b, t], info[:, t, col].rearrange("p a c -> p (a c)"),
                                           start=(t == 0), stop=(t == NT - 1))
                return ins

            def slot_numbers(u, done):
                nc.vector.tensor_reduce(wslot[:, u:u + 1], bank[:, 7, 3:NCOL], AX_X, ALU.add).then_inc(done, 1)
                nc.vector.tensor_scalar(idx[:, u], bank[:, 7, 1:3], bank[:, 7, 0:1], float(NONE),
                                        ALU.add, ALU.add).then_inc(done, 1)

            def gather(b, u):
                nc.gpsimd.sem_inc(pool_steps, 1)
                return nc.gpsimd.indirect_dma_start(
                    gathered[:, b], None, tokens, bass.IndirectOffsetOnAxis(ap=idx[:, u, 0:1], axis=0),
                    bounds_check=T - 1, oob_is_err=False)

            def scatter(b, u):
                nc.gpsimd.sem_inc(pool_steps, 1)
                return nc.gpsimd.indirect_dma_start(
                    rows, bass.IndirectOffsetOnAxis(ap=idx[:, u, 1:2], axis=0), eo[:, b], None,
                    bounds_check=TOP * T - 1, oob_is_err=False)

            def turn(b, g):
                for k in range(KD):
                    ins = nc.tensor.transpose(bank[:, b, k * P:(k + 1) * P], gathered[:, g, k * P:(k + 1) * P], ident[:])
                return ins

            def gate_up(b, u):
                for half in range(2):
                    for k in range(KD):
                        ins = nc.tensor.matmul(bank[:, 2 + b, half * P:(half + 1) * P], gate_w(ring[:, u], half, k),
                                               slotT[:, b, k], start=(k == 0), stop=(k == KD - 1))
                return ins

            def groups(eng, step, ahead):
                for m in range(-ahead, RING):
                    step(0, m)
                with eng.Fori(1, E // RING - 1) as q:
                    for m in range(RING):
                        step(q, m)
                for m in range(RING + 1):
                    step(E // RING - 1, m)

            with nc.Block() as block:
                @block.sync
                def _(sp):
                    def load(q, m):
                        sp.wait_ge(eo_done, item(q, m) - RING + 1)
                        sp.dma_start(ring[:, m], w_expert[column(q, m)].rearrange("a p n -> p (a n)")
                                     ).then_inc(ld_e[m], 16)

                    with sp.Fori(1, E // RING) as q:
                        for m in range(RING):
                            load(q, m)

                @block.gpsimd
                def _(pool):
                    pool.wait_ge(tokens_stored, 16)

                    def step(q, m):
                        if exists(q, m + 5):
                            n, u = item(q, m + 5), (m + 5) % RING
                            pool.wait_ge(idx_ready, n * 2 + 2)
                            at_least(pool, sT_done, n - GB + 1)
                            gather(u % GB, u).then_inc(ld_g[u % GB], 16)
                        if exists(q, m - 1):
                            n, u = item(q, m - 1), (m - 1) % RING
                            pool.wait_ge(eo_ready, n + 1)
                            scatter(u % EB, u).then_inc(st_e[u % EB], 16)

                    groups(pool, step, 6)
                    for b in range(EB):
                        pool.wait_ge(st_e[b], 16 * (E // EB))

                @block.vector
                def _(vec):
                    def step(q, m):
                        if exists(q, m):
                            n, u = item(q, m), m % RING
                            vec.wait_ge(sil_ready, n + 1)
                            at_least(vec, eo_done, n - 1)
                            nc.vector.tensor_tensor(hid[:, u % 2], sil[:, u % 2], bank[:, 2 + u % 2, P:2 * P],
                                                    ALU.mult).then_inc(hid_ready, 1)
                        if exists(q, m + 2):
                            n, u = item(q, m + 2), (m + 2) % RING
                            vec.wait_ge(sT_done, n + 1)
                            at_least(vec, gu_done, n - 1)
                            nc.vector.tensor_copy(slotT[:, u % 2], bank[:, u % 2].rearrange("p (k s) -> p k s", k=KD)
                                                  ).then_inc(sT_ready, 1)
                        if exists(q, m + 5):
                            n, u = item(q, m + 5), (m + 5) % RING
                            vec.wait_ge(idx_done, n + 1)
                            at_least(vec, st_e[u % EB], fours(q, m + 5) * 16 - 16)
                            slot_numbers(u, idx_ready)
                        if exists(q, m + 6):
                            n, u = item(q, m + 6), (m + 6) % RING
                            at_least(vec, idx_done, n - 1)
                            col = column(q, m + 6)
                            pick_slots(u % 2, jtab[:, col], col).then_inc(picked, 1)

                    groups(vec, step, 6)

                @block.scalar
                def _(act):
                    def step(q, m):
                        if exists(q, m):
                            n, u = item(q, m), m % RING
                            act.wait_ge(gu_done, n + 1)
                            at_least(act, hid_ready, n - 1)
                            nc.scalar.activation(sil[:, u % 2], bank[:, 2 + u % 2, 0:P], ACT.Silu).then_inc(sil_ready, 1)
                        if exists(q, m - 1):
                            n, u = item(q, m - 1), (m - 1) % RING
                            act.wait_ge(eo_done, n + 1)
                            at_least(act, st_e[u % EB], fours(q, m - 1) * 16)
                            nc.scalar.activation(eo[:, u % EB], bank[:, 4 + u % 2], ACT.Copy,
                                                 scale=wslot[:, u:u + 1]).then_inc(eo_ready, 1)

                    groups(act, step, 0)

                @block.tensor
                def _(pe):
                    def step(q, m):
                        if exists(q, m):
                            n, u = item(q, m), m % RING
                            pe.wait_ge(sT_ready, n + 1)
                            pe.wait_ge(ld_e[u], q * 16 + 16)
                            at_least(pe, hid_ready, n - 1)
                            gate_up(u % 2, u).then_inc(gu_done, 1)
                        if exists(q, m - 1):
                            n, u = item(q, m - 1), (m - 1) % RING
                            pe.wait_ge(hid_ready, n + 1)
                            at_least(pe, eo_ready, n - 1)
                            nc.tensor.matmul(bank[:, 4 + u % 2], hid[:, u % 2], down_w(ring[:, u]),
                                             start=True, stop=True).then_inc(eo_done, 1)
                        if exists(q, m + 2):
                            n, u = item(q, m + 2), (m + 2) % RING
                            pe.wait_ge(ld_g[u % GB], fours(q, m + 2) * 16 + 16)
                            at_least(pe, sT_ready, n - 1)
                            turn(u % 2, u % GB).then_inc(sT_done, 1)
                        if exists(q, m + 5):
                            n, u = item(q, m + 5), (m + 5) % RING
                            pe.wait_ge(picked, n + 1)
                            at_least(pe, idx_ready, n * 2)
                            index_products(u % 2, column(q, m + 5)).then_inc(idx_done, 1)

                    groups(pe, step, 6)

            ov_load, ov_picked, ov_idx_done = semp("ov_load"), semp("ov_picked"), semp("ov_idx_done")
            ov_idx, ov_gathered, ov_turned = semp("ov_idx"), semp("ov_gathered"), semp("ov_turned")
            ov_sT, ov_gu, ov_sil, ov_hid = semp("ov_sT"), semp("ov_gu"), semp("ov_sil"), semp("ov_hid")
            ov_out, ov_scaled, ov_stored = semp("ov_out"), semp("ov_scaled"), semp("ov_stored")
            sh_gu, sh_sil, sh_hid, sh_out = semp("sh_gu"), semp("sh_sil"), semp("sh_hid"), semp("sh_out")
            ld_p = [semp(f"ld_p{t}") for t in range(NT)]
            sh_added, summed, y_ready, y_stored = semp("sh_added"), semp("summed"), semp("y_ready"), semp("y_stored")

            with nc.Block() as block:
                @block.sync
                def _(sp):
                    count = sp.value_load(over_n[0:1, 0:1], min_val=1, max_val=OVER)
                    with sp.Fori(0, count) as o:
                        e = sp.value_load(over_e[0:1, bass.ds(o, 1)], min_val=0, max_val=E - 1)
                        sp.wait_ge(ov_picked, o + 1)
                        sp.dma_start(ring[:, 0], w_expert[bass.ds(e, 1)].rearrange("a p n -> p (a n)")
                                     ).then_inc(ov_load, 16)
                    sp.wait_ge(ov_stored, count * 16)
                    for t in range(NT):
                        sp.dma_start(part[:, t], rows.rearrange("(k t p) d -> t p k d", k=TOP, t=NT)[t]
                                     ).then_inc(ld_p[t], 16)
                    for t in range(NT):
                        sp.wait_ge(y_ready, t + 1)
                        sp.dma_start(out[t * P:(t + 1) * P], total[:, t]).then_inc(y_stored, 16)
                    sp.wait_ge(y_stored, 16 * NT)

                @block.gpsimd
                def _(pool):
                    count = pool.value_load(over_n[0:1, 0:1], min_val=1, max_val=OVER)
                    with pool.Fori(0, count) as o:
                        pool.wait_ge(ov_idx, o * 2 + 2)
                        gather(0, 0).then_inc(ov_gathered, 16)
                        pool.wait_ge(ov_scaled, o + 1)
                        scatter(0, 0).then_inc(ov_stored, 16)

                @block.vector
                def _(vec):
                    count = vec.value_load(over_n[0:1, 0:1], min_val=1, max_val=OVER)
                    with vec.Fori(0, count) as o:
                        e = vec.value_load(over_e[0:1, bass.ds(o, 1)], min_val=0, max_val=E - 1)
                        pick_slots(0, jtab[:, bass.ds(o + E, 1)], bass.ds(e, 1)).then_inc(ov_picked, 1)
                        vec.wait_ge(ov_idx_done, o + 1)
                        slot_numbers(0, ov_idx)
                        vec.wait_ge(ov_turned, o + 1)
                        nc.vector.tensor_copy(slotT[:, 0], bank[:, 0].rearrange("p (k s) -> p k s", k=KD)
                                              ).then_inc(ov_sT, 1)
                        vec.wait_ge(ov_sil, o + 1)
                        nc.vector.tensor_tensor(hid[:, 0], sil[:, 0], bank[:, 2, P:2 * P], ALU.mult).then_inc(ov_hid, 1)
                        vec.wait_ge(ov_stored, o * 16 + 16)
                    vec.wait_ge(sh_sil, 1)
                    nc.vector.tensor_tensor(shid[:], ssil[:], bank[:, 3], ALU.mult).then_inc(sh_hid, 1)
                    for t in range(NT):
                        vec.wait_ge(sh_out, t + 1)
                        nc.vector.scalar_tensor_tensor(out=xt[:, t], in0=bank[:, 4 + t], scalar=sgate[:, t:t + 1],
                                                       in1=xt[:, t], op0=ALU.mult, op1=ALU.add).then_inc(sh_added, 1)
                    for t in range(NT):
                        vec.wait_ge(ld_p[t], 16)
                        nc.vector.tensor_reduce(xn[:, t], part[:, t].rearrange("p k d -> p d k"), AX_X, ALU.add
                                                ).then_inc(summed, 1)
                        vec.wait_ge(summed, t + 1)
                        vec.wait_ge(sh_added, t + 1)
                        nc.vector.tensor_tensor(total[:, t], xn[:, t], xt[:, t], ALU.add).then_inc(y_ready, 1)

                @block.scalar
                def _(act):
                    count = act.value_load(over_n[0:1, 0:1], min_val=1, max_val=OVER)
                    with act.Fori(0, count) as o:
                        act.wait_ge(ov_gu, o + 1)
                        nc.scalar.activation(sil[:, 0], bank[:, 2, 0:P], ACT.Silu).then_inc(ov_sil, 1)
                        act.wait_ge(ov_out, o + 1)
                        nc.scalar.activation(eo[:, 0], bank[:, 4], ACT.Copy, scale=wslot[:, 0:1]).then_inc(ov_scaled, 1)
                    act.wait_ge(sh_gu, 1)
                    nc.scalar.activation(ssil[:], bank[:, 2], ACT.Silu).then_inc(sh_sil, 1)

                @block.tensor
                def _(pe):
                    count = pe.value_load(over_n[0:1, 0:1], min_val=1, max_val=OVER)
                    with pe.Fori(0, count) as o:
                        e = pe.value_load(over_e[0:1, bass.ds(o, 1)], min_val=0, max_val=E - 1)
                        pe.wait_ge(ov_picked, o + 1)
                        index_products(0, bass.ds(e, 1)).then_inc(ov_idx_done, 1)
                        pe.wait_ge(ov_gathered, o * 16 + 16)
                        turn(0, 0).then_inc(ov_turned, 1)
                        pe.wait_ge(ov_sT, o + 1)
                        pe.wait_ge(ov_load, o * 16 + 16)
                        gate_up(0, 0).then_inc(ov_gu, 1)
                        pe.wait_ge(ov_hid, o + 1)
                        nc.tensor.matmul(bank[:, 4], hid[:, 0], down_w(ring[:, 0]),
                                         start=True, stop=True).then_inc(ov_out, 1)
                    pe.wait_ge(ov_scaled, count)
                    for half in range(2):
                        for k in range(KD):
                            ins = nc.tensor.matmul(bank[:, 2 + half], gate_w(wsh_sb, half, k), xT[:, k],
                                                   start=(k == 0), stop=(k == KD - 1))
                    ins.then_inc(sh_gu, 1)
                    pe.wait_ge(sh_hid, 1)
                    for t in range(NT):
                        nc.tensor.matmul(bank[:, 4 + t], shid[:, t * P:(t + 1) * P], down_w(wsh_sb),
                                         start=True, stop=True).then_inc(sh_out, 1)


def kernel(**inputs):
    import numpy as np
    import concourse.bacc as bacc
    from concourse.bass_utils import run_bass_kernel_spmd

    a = {k: np.asarray(v) for k, v in inputs.items()}
    x = a["x"].reshape(-1, a["x"].shape[-1])
    D = x.shape[1]
    KD = D // P
    ctx = a["ctx_2048"]
    B, L, _ = ctx.shape
    NCH = -(-L // P)
    rows = np.zeros((B, NCH * P, D), ctx.dtype)
    rows[:, :L] = ctx
    rows = rows.reshape(B, NCH, P, D)
    cols = rows.reshape(B, NCH, P, KD, P).transpose(0, 1, 4, 3, 2).reshape(B, NCH, P, KD * P)
    mask = np.zeros((B, NCH * P), np.bool_)
    mask[:, :L] = a["mask_BxS2_bk0"]

    def by_k(w):
        return w.reshape(KD, P, -1).transpose(1, 0, 2)

    def gated(gate_up, down):
        lead = gate_up.shape[:-2]
        g = gate_up.reshape(*lead, 2, P, KD, P)
        n = len(lead)
        g = g.transpose(*range(n), n + 3, n + 2, n, n + 1).reshape(*lead, P, KD * 2 * P)
        return np.concatenate([g, np.swapaxes(down, -1, -2)], axis=-1)

    arrays = {
        "x": x, "ctx_rows": rows, "ctx_cols": cols, "mask": mask,
        "w_qkv": by_k(a["L0_attn_w_qkv"]), "w_out": by_k(a["L0_attn_w_out"]),
        "w_router": by_k(np.concatenate([a["L0_ffn_router_w"], a["L0_ffn_shared_expert_gate_w"]], axis=0).T),
        "w_shared": gated(np.concatenate([a["L0_ffn_shared_gate_w"], a["L0_ffn_shared_up_w"]], axis=0),
                          a["L0_ffn_shared_down_w"]),
        "w_expert": gated(a["L0_ffn_gate_up_proj"], a["L0_ffn_down_proj"]),
    }
    nc = bacc.Bacc("TRN2", target_bir_lowering=False, num_devices=1)
    given, args = {}, []
    for name, arr in arrays.items():
        arr = np.ascontiguousarray(arr)
        given[f"in_{name}"] = arr
        args.append(nc.dram_tensor(f"in_{name}", arr.shape, mybir.dt.from_np(arr.dtype), kind="ExternalInput").ap())
    args.append(nc.dram_tensor("out_y", x.shape, F32, kind="ExternalOutput").ap())
    args.append(nc.dram_tensor("tokens", x.shape, F32, kind="Internal").ap())
    args.append(nc.dram_tensor("rows", (8 * x.shape[0], D), F32, kind="Internal").ap())
    build_program(nc, *args)
    res = run_bass_kernel_spmd(nc, [given], core_ids=[0])
    return res.results[0]["out_y"].reshape(a["x"].shape)
```

```python
from contextlib import ExitStack

import concourse.bass as bass
from concourse import mybir

ALU = mybir.AluOpType
ACT = mybir.ActivationFunctionType
F32 = mybir.dt.float32
F32R = mybir.dt.float32r
BF16 = mybir.dt.bfloat16
U8 = mybir.dt.uint8
I32 = mybir.dt.int32
AX_X = mybir.AxisListType.X

P = 128
S = 64
HB = P // S
DROPPED = 2.0 ** 104
NEG_CAUSAL = 1.0e10
EPS = 1e-5


def build_program(nc, x, ctx_both, mask, consts, w_qkv, w_out, w_router, w_shared, w_expert, out, tokens, rows):
    T, D = x.shape
    NT = T // P
    KD = D // P
    B = T // S
    NCH = ctx_both.shape[0] // B
    FEW = 4
    NCONST = consts.shape[1]
    HEADS, DH = 16, D // 16
    RG = P // DH
    NG = HEADS // RG
    E = w_expert.shape[0]
    I = P
    SC_CTX = float(D) ** -0.5
    SC_HEAD = float(DH) ** -0.5
    EO = E + 1
    RING = 8
    GROUP = 16
    TOP = 8
    SL = 112
    OVER = T * TOP // SL
    MORE = -(-T // SL) - 1
    SOME = (56, 80)
    ITEMS = E + OVER
    NONE = 8192
    NCOL = 6
    GB, EB, DB = 4, 4, 4
    CONSTS = 8
    WE = KD * 2 * I + D
    assert E % GROUP == 0 and GROUP % RING == 0 and RING % GB == 0 and RING % EB == 0 and TOP * T <= NONE

    with ExitStack() as st:
        def sb(name, shape, dt=F32):
            return st.enter_context(nc.sbuf_tensor(name, shape, dt))

        def sem(name):
            return st.enter_context(nc.semaphore(name))

        bank = st.enter_context(nc.psum_tensor("bank", [P, 8, 512], F32))

        ident = sb("ident", [P, P])
        xt = sb("xt", [P, NT, D])
        xn = sb("xn", [P, NT, D])
        xT = sb("xT", [P, KD, T])
        stats = sb("stats", [P, NT, 6])
        mv = sb("mv", [P, NT, 2])
        var = sb("var", [P, NT])
        std = sb("std", [P, NT])
        rstd = sb("rstd", [P, NT])
        wr_sb = sb("wr_sb", [P, KD, EO])
        wsh_sb = sb("wsh_sb", [P, WE])
        places = sb("places", [P, GROUP, WE])
        flat = places[:].rearrange("p u n -> p (u n)")
        LAST = 2
        last = sb("last", [P, LAST, WE])
        ld_e = [sem(f"ld_e{u}") for u in range(RING)]
        tokens_stored = sem("tokens_stored")
        early = ExitStack()
        causal = early.enter_context(nc.sbuf_tensor("causal", [P, HEADS, S], F32))
        LATE = GROUP - 3 * D * KD // WE
        wqkv_sb = flat[:, LATE * WE:GROUP * WE].rearrange("p (k n) -> p k n", k=KD)

        ln_step, std_ready, xn_ready = sem("ln_step"), sem("std_ready"), sem("xn_ready")
        xT_done, xT_ready = sem("xT_done"), sem("xT_ready")
        LN_STEPS = 2 * NT + 2

        def norm_stats(j):
            nc.vector.bn_stats(stats[:, j], xt[:, j]).then_inc(ln_step, 1)

        def norm_tiles(vec, h):
            base = LN_STEPS * h
            vec.wait_ge(ln_step, base + NT)
            for j in range(NT):
                nc.vector.bn_aggr(mv[:, j], stats[:, j]).then_inc(ln_step, 1)
            vec.wait_ge(ln_step, base + 2 * NT)
            nc.vector.tensor_scalar(var[:], mv[:, :, 1], EPS, None, ALU.add).then_inc(ln_step, 1)
            vec.wait_ge(std_ready, h + 1)
            nc.vector.reciprocal(rstd[:], std[:]).then_inc(ln_step, 1)
            vec.wait_ge(ln_step, base + LN_STEPS)
            for j in range(NT):
                nc.vector.tensor_scalar(xn[:, j], xt[:, j], mv[:, j, 0:1], rstd[:, j:j + 1],
                                        ALU.subtract, ALU.mult).then_inc(xn_ready, 1)

        def norm_roots(act, h):
            act.wait_ge(ln_step, LN_STEPS * h + 2 * NT + 1)
            nc.scalar.activation(std[:], var[:], ACT.Sqrt).then_inc(std_ready, 1)

        def turn_tiles(pe, h, first):
            for j in range(NT):
                pe.wait_ge(xn_ready, NT * h + j + 1)
                if j >= 2:
                    pe.wait_ge(xT_ready, NT * h + j - 1)
                for k in range(KD):
                    ins = nc.tensor.transpose(bank[:, first + j % 2, k * P:(k + 1) * P],
                                              xn[:, j, k * P:(k + 1) * P], ident[:])
                ins.then_inc(xT_done, 1)

        def copy_turned(act, h, first):
            for j in range(NT):
                act.wait_ge(xT_done, NT * h + j + 1)
                nc.scalar.activation(xT[:, :, j * P:(j + 1) * P],
                                     bank[:, first + j % 2].rearrange("p (k t) -> p k t", k=KD),
                                     ACT.Copy).then_inc(xT_ready, 1)

        with ExitStack() as ph:
            def sbp(name, shape, dt=F32):
                return ph.enter_context(nc.sbuf_tensor(name, shape, dt))

            BC = B * NCH
            REST = NCH - FEW
            cset = HB * FEW * 2 * D
            assert (cset + REST * 2 * D) <= LATE * WE
            cbuf = [sbp("cbuf", [P, cset])[:].rearrange("p (h c n) -> p h c n", h=HB, c=FEW),
                    flat[:, 0:cset].rearrange("p (h c n) -> p h c n", h=HB, c=FEW)]
            crest = flat[:, cset:cset + REST * 2 * D].rearrange("p (c n) -> p c n", c=REST)
            prob = sbp("prob", [P, 2, FEW * P])
            probT = sbp("probT", [P, 2, FEW, P])
            prest = sbp("prest", [P, REST * P])
            prestT = sbp("prestT", [P, REST, P])
            kc = sbp("kc", [BC, NCONST])
            k_before, k_same = kc[:, 0:BC], kc[:, BC:2 * BC]
            k_place = kc[:, 2 * BC:3 * BC]
            k_half = kc[:, 3 * BC:3 * BC + P]
            k_pair = kc[:, 3 * BC + P:3 * BC + P + NT]
            k_batch = kc[:, 3 * BC + P + NT:3 * BC + P + NT + B]
            k_row = kc[:, NCONST - 2:NCONST - 1]
            k_chunk = kc[:, NCONST - 1:NCONST]
            mrow = sbp("mrow", [BC, P], U8)
            mneg = sbp("mneg", [BC, P], BF16)
            kept = sbp("kept", [BC, 1])
            keptp = sbp("keptp", [BC, P])
            before = sbp("before", [BC, 2])
            place = sbp("place", [BC, 4])
            sel = sbp("sel", [BC, BC])
            selb = sbp("selb", [BC, BC], BF16)
            selw = sbp("selw", [BC, B, FEW, S], BF16)
            order = sbp("order", [1, BC], I32)
            more_n = sbp("more_n", [1, NT], I32)
            anyv = sbp("anyv", [P, NT])
            rmax = sbp("rmax", [P, NT, 2])
            nmax = sbp("nmax", [P, NT])
            rsum = sbp("rsum", [P, NT, 2])
            rall = sbp("rall", [P, NT])
            rinv = sbp("rinv", [P, NT])
            gain = sbp("gain", [P, NT])

            ld_x, ld_mask = sem("ld_x"), sem("ld_mask")
            ld_w, ld_wf = sem("ld_w"), sem("ld_wf")
            ld_cols = [[sem(f"ld_cols{b}_{half}") for half in range(HB)] for b in range(2)]
            ld_rows = [[sem(f"ld_rows{b}_{half}") for half in range(HB)] for b in range(2)]
            ident_ready, zeroed = sem("ident_ready"), sem("zeroed")
            causal_ready = sem("causal_ready")
            kept_ready, kept_copies, before_done = sem("kept_ready"), sem("kept_copies"), sem("before_done")
            place_step, sel_ready, selw_ready = sem("place_step"), sem("sel_ready"), sem("selw_ready")
            order_done, order_ready = sem("order_done"), sem("order_ready")
            scores_done, max_ready, nmax_ready = sem("scores_done"), sem("max_ready"), sem("nmax_ready")
            exp_ready, pT_done, pT_copied = sem("exp_ready"), sem("pT_done"), sem("pT_copied")
            pv_done, rinv_ready, gain_ready = sem("pv_done"), sem("rinv_ready"), sem("gain_ready")
            x1_ready = sem("x1_ready")
            r_load = [sem(f"r_load{j}") for j in range(NT)]
            r_scores = [sem(f"r_scores{j}") for j in range(NT)]
            r_max = [sem(f"r_max{j}") for j in range(NT)]
            r_exp = [sem(f"r_exp{j}") for j in range(NT)]
            r_pT = [sem(f"r_pT{j}") for j in range(NT)]
            r_copied = [sem(f"r_copied{j}") for j in range(NT)]
            r_pv = [sem(f"r_pv{j}") for j in range(NT)]

            def further(eng, counts, j):
                return eng.If(counts[j] > FEW)

            def load_counts(eng):
                eng.wait_ge(order_ready, 2)
                return [eng.value_load(more_n[0:1, j:j + 1], min_val=0, max_val=NCH) for j in range(NT)]

            def load_chunks(eng, j, half, part):
                for c in range(FEW):
                    n = (HB * j + half) * NCH + c
                    r = eng.value_load(order[0:1, n:n + 1], min_val=0, max_val=BC - 1)
                    eng.dma_start(cbuf[j % 2][:, half, c, part * D:(part + 1) * D],
                                  ctx_both[bass.ds(r, 1), :, part * D:(part + 1) * D].rearrange("a p n -> p (a n)")
                                  ).then_inc((ld_rows if part else ld_cols)[j % 2][half], 16)

            def load_further(sp, counts, j):
                with further(sp, counts, j):
                    for turn in range(2 * HB):
                        if turn:
                            sp.wait_ge(r_scores[j] if turn <= HB else r_pv[j], turn if turn <= HB else turn - HB)
                        half = turn % HB
                        for c in range(FEW, NCH):
                            r = sp.value_load(order[0:1, (HB * j + half) * NCH + c:(HB * j + half) * NCH + c + 1],
                                              min_val=0, max_val=BC - 1)
                            sp.dma_start(crest[:, c - FEW], ctx_both[bass.ds(r, 1)].rearrange("a p n -> p (a n)")
                                         ).then_inc(r_load[j], 16)
                    sp.wait_ge(r_pv[j], HB)

            with nc.Block() as block:
                @block.sync
                def _(sp):
                    sp.dma_start(mrow[:], mask).then_inc(ld_mask, 16)
                    sp.dma_start(kc[:], consts).then_inc(ld_mask, 16)
                    for t in range(NT):
                        sp.dma_start(xt[:, t], x[t * P:(t + 1) * P]).then_inc(ld_x, 16)
                    sp.dma_start(wqkv_sb[:, 0:KD // 2], w_qkv[:, 0:KD // 2]).then_inc(ld_w, 16)
                    counts = load_counts(sp)
                    load_chunks(sp, 0, 0, 0)
                    for j in range(NT):
                        if j + 1 < NT:
                            if j >= 1:
                                sp.wait_ge(scores_done, HB * j)
                            load_chunks(sp, j + 1, 0, 0)
                        if j >= 2:
                            sp.wait_ge(pv_done, j - 1)
                        load_chunks(sp, j, 0, 1)
                        if j:
                            load_further(sp, counts, j - 1)
                    sp.wait_ge(scores_done, HB * NT)
                    sp.dma_start(wqkv_sb[:, KD // 2:KD], w_qkv[:, KD // 2:KD]).then_inc(ld_w, 16)
                    load_further(sp, counts, NT - 1)

                @block.gpsimd
                def _(pool):
                    nc.gpsimd.memset(ident[:], 0.0).then_inc(zeroed, 1)
                    nc.gpsimd.memset(rsum[:], 0.0).then_inc(zeroed, 1)
                    pool.wait_ge(zeroed, 1)
                    nc.gpsimd.affine_select(out=ident[:], in_=ident[:], compare_op=ALU.not_equal, fill=1.0,
                                            base=0, pattern=[[-1, P]], channel_multiplier=1).then_inc(ident_ready, 1)
                    for half in range(HB):
                        nc.gpsimd.memset(causal[half * S:(half + 1) * S], 0.0).then_inc(zeroed, 1)
                        pool.wait_ge(zeroed, half + 3)
                        nc.gpsimd.affine_select(out=causal[half * S:(half + 1) * S],
                                                in_=causal[half * S:(half + 1) * S],
                                                compare_op=ALU.is_ge, fill=-NEG_CAUSAL, base=0,
                                                pattern=[[0, HEADS], [-1, S]],
                                                channel_multiplier=1).then_inc(causal_ready, 1)
                    pool.wait_ge(order_ready, 2)
                    load_chunks(pool, 0, 1, 0)
                    for j in range(NT):
                        if j + 1 < NT:
                            if j >= 1:
                                pool.wait_ge(scores_done, HB * j)
                            load_chunks(pool, j + 1, 1, 0)
                        if j >= 2:
                            pool.wait_ge(pv_done, j - 1)
                        load_chunks(pool, j, 1, 1)

                @block.scalar
                def _(act):
                    norm_roots(act, 0)
                    copy_turned(act, 0, 2)
                    counts = load_counts(act)
                    act.wait_ge(zeroed, 2)
                    for j in range(NT):
                        b = j % 2
                        act.wait_ge(nmax_ready, j + 1)
                        if j >= 2:
                            act.wait_ge(pT_done, j - 1)
                        nc.scalar.activation(prob[:, b], bank[:, b], ACT.Exp, bias=nmax[:, j:j + 1], scale=SC_CTX,
                                             accum_out=rsum[:, j, 0:1]).then_inc(exp_ready, 1)
                        with further(act, counts, j):
                            nc.scalar.activation(prest[:], bank[:, 2:5].rearrange("p b n -> p (b n)")[:, 0:REST * P],
                                                 ACT.Exp, bias=nmax[:, j:j + 1], scale=SC_CTX,
                                                 accum_out=rsum[:, j, 1:2]).then_inc(r_exp[j], 1)
                            for g in range(0, REST, 4):
                                n = min(4, REST - g)
                                act.wait_ge(r_pT[j], g // 4 + 1)
                                nc.scalar.activation(prestT[:, g:g + n],
                                                     bank[:, 5, 0:n * P].rearrange("p (c q) -> p c q", c=n),
                                                     ACT.Copy).then_inc(r_copied[j], 1)
                        act.wait_ge(pT_done, j + 1)
                        if j >= 2:
                            act.wait_ge(pv_done, j - 1)
                        nc.scalar.activation(probT[:, b], bank[:, 5].rearrange("p (c q) -> p c q", c=FEW),
                                             ACT.Copy).then_inc(pT_copied, 1)

                @block.vector
                def _(vec):
                    vec.wait_ge(ld_mask, 32)
                    nc.vector.tensor_reduce(kept[:], mrow[:], AX_X, ALU.max).then_inc(kept_ready, 1)
                    nc.vector.tensor_scalar(mneg[:], mrow[:], -1.0, DROPPED, ALU.add, ALU.mult
                                            ).then_inc(kept_copies, 1)
                    vec.wait_ge(kept_ready, 1)
                    nc.vector.tensor_scalar(keptp[:], k_half, kept[:, 0:1], None, ALU.mult).then_inc(kept_copies, 1)
                    n = [0]

                    def chain(ins):
                        n[0] += 1
                        ins.then_inc(place_step, 1)
                        vec.wait_ge(place_step, n[0])

                    vec.wait_ge(before_done, 1)
                    chain(nc.vector.tensor_copy(before[:], bank[0:BC, 4, 0:2]))
                    chain(nc.vector.tensor_tensor(place[:, 0:1], before[:, 1:2], k_chunk, ALU.add))
                    chain(nc.vector.scalar_tensor_tensor(out=place[:, 1:2], in0=before[:, 0:1], scalar=-2.0,
                                                         in1=place[:, 0:1], op0=ALU.mult, op1=ALU.add))
                    chain(nc.vector.tensor_scalar(place[:, 2:3], kept[:], -1.0, 1.0, ALU.mult, ALU.add))
                    chain(nc.vector.scalar_tensor_tensor(out=place[:, 3:4], in0=place[:, 1:2], scalar=place[:, 2:3],
                                                         in1=before[:, 0:1], op0=ALU.mult, op1=ALU.add))
                    nc.vector.tensor_scalar(sel[:], k_place, place[:, 3:4], None, ALU.is_equal).then_inc(sel_ready, 1)
                    vec.wait_ge(sel_ready, 1)
                    vec.wait_ge(order_done, 1)
                    nc.vector.tensor_copy(order[:], bank[0:1, 4, 0:BC]).then_inc(order_ready, 1)
                    nc.vector.tensor_reduce(more_n[:], bank[0:1, 4, BC:BC + B].rearrange("o (j h) -> o j h", h=HB),
                                            AX_X, ALU.max).then_inc(order_ready, 1)
                    nc.vector.tensor_scalar(anyv[:], bank[:, 4, BC + B:BC + B + NT], 1.0, None, ALU.min
                                            ).then_inc(order_ready, 1)
                    nc.vector.tensor_copy(selb[:], sel[:]).then_inc(selw_ready, 1)
                    nc.vector.tensor_copy(selw[:], sel[:].rearrange("r (b c) -> r b c", b=B)[:, :, 0:FEW].unsqueeze(3)
                                          .broadcast_to([BC, B, FEW, S])).then_inc(selw_ready, 1)
                    vec.wait_ge(ld_x, 16 * NT)
                    for j in range(NT):
                        norm_stats(j)
                    norm_tiles(vec, 0)
                    counts = load_counts(vec)
                    vec.wait_ge(order_ready, 3)
                    for j in range(NT):
                        b = j % 2
                        vec.wait_ge(scores_done, HB * (j + 1))
                        nc.vector.tensor_reduce(rmax[:, j, 0:1], bank[:, b], AX_X, ALU.max).then_inc(max_ready, 1)
                        vec.wait_ge(max_ready, j + 1)
                        with further(vec, counts, j):
                            vec.wait_ge(r_scores[j], HB)
                            nc.vector.tensor_reduce(rmax[:, j, 1:2], bank[:, 2:5].rearrange("p b n -> p (b n)")[:, 0:REST * P],
                                                    AX_X, ALU.max).then_inc(r_max[j], 1)
                            vec.wait_ge(r_max[j], 1)
                            nc.vector.tensor_tensor(rmax[:, j, 0:1], rmax[:, j, 0:1], rmax[:, j, 1:2], ALU.max
                                                    ).then_inc(r_max[j], 1)
                            vec.wait_ge(r_max[j], 2)
                        nc.vector.tensor_scalar(nmax[:, j:j + 1], rmax[:, j, 0:1], -SC_CTX, None,
                                                ALU.mult).then_inc(nmax_ready, 1)
                        vec.wait_ge(exp_ready, j + 1)
                        with further(vec, counts, j):
                            vec.wait_ge(r_exp[j], 1)
                        nc.vector.tensor_reduce(rall[:, j:j + 1], rsum[:, j], AX_X, ALU.add).then_inc(gain_ready, 1)
                        vec.wait_ge(gain_ready, 3 * j + 1)
                        nc.vector.reciprocal(rinv[:, j:j + 1], rall[:, j:j + 1]).then_inc(gain_ready, 1)
                        vec.wait_ge(gain_ready, 3 * j + 2)
                        nc.vector.tensor_tensor(gain[:, j:j + 1], rinv[:, j:j + 1], anyv[:, j:j + 1],
                                                ALU.mult).then_inc(gain_ready, 1)
                        vec.wait_ge(gain_ready, 3 * j + 3)
                        vec.wait_ge(pv_done, j + 1)
                        nc.vector.scalar_tensor_tensor(out=xt[:, j], in0=bank[:, 6 + j % 2], scalar=gain[:, j:j + 1],
                                                       in1=xt[:, j], op0=ALU.mult, op1=ALU.add).then_inc(x1_ready, 1)
                        vec.wait_ge(x1_ready, j + 1)
                        norm_stats(j)

                @block.tensor
                def _(pe):
                    pe.wait_ge(ld_mask, 32)
                    pe.wait_ge(kept_ready, 1)
                    nc.tensor.matmul(bank[0:BC, 4, 0:1], k_before, kept[:], start=True, stop=True)
                    nc.tensor.matmul(bank[0:BC, 4, 1:2], k_same, kept[:], start=True, stop=True).then_inc(before_done, 1)
                    pe.wait_ge(sel_ready, 1)
                    pe.wait_ge(kept_copies, 2)
                    nc.tensor.matmul(bank[0:1, 4, 0:BC], k_row, sel[:], start=True, stop=True)
                    nc.tensor.matmul(bank[0:1, 4, BC:BC + B], kept[:], k_batch, start=True, stop=True)
                    nc.tensor.matmul(bank[:, 4, BC + B:BC + B + NT], keptp[:], k_pair, start=True, stop=True
                                     ).then_inc(order_done, 1)
                    pe.wait_ge(ident_ready, 1)
                    turn_tiles(pe, 0, 2)
                    counts = load_counts(pe)
                    pe.wait_ge(order_ready, 3)
                    pe.wait_ge(xT_ready, NT)
                    pe.wait_ge(selw_ready, 2)

                    def chunk_scores(out_ap, j, half, c, cols):
                        b = HB * j + half
                        for k in range(KD):
                            nc.tensor.matmul(out_ap, xT[:, k, b * S:(b + 1) * S], cols[:, k * P:(k + 1) * P],
                                             start=(k == 0), stop=False)
                        chosen = (selw[:, b, c] if c < FEW
                                  else selb[:, b * NCH + c:b * NCH + c + 1].broadcast_to([BC, S]))
                        return nc.tensor.matmul(out_ap, chosen, mneg[:], start=False, stop=True)

                    def scores(j):
                        if j >= 2:
                            pe.wait_ge(exp_ready, j - 1)
                        for half in range(HB):
                            pe.wait_ge(ld_cols[j % 2][half], 16 * FEW * (j // 2 + 1))
                            for c in range(FEW):
                                ins = chunk_scores(bank[half * S:(half + 1) * S, j % 2, c * P:(c + 1) * P],
                                                   j, half, c, cbuf[j % 2][:, half, c])
                            ins.then_inc(scores_done, 1)

                    def further_scores(j):
                        with further(pe, counts, j):
                            for half in range(HB):
                                pe.wait_ge(r_load[j], 16 * REST * (half + 1))
                                for c in range(REST):
                                    ins = chunk_scores(bank[half * S:(half + 1) * S, 2 + c // 4, (c % 4) * P:(c % 4 + 1) * P],
                                                       j, half, FEW + c, crest[:, c])
                                ins.then_inc(r_scores[j], 1)

                    def sum_chunk(j, half, pt, rws, start, stop):
                        return nc.tensor.matmul(bank[half * S:(half + 1) * S, 6 + j % 2], pt[:, half * S:(half + 1) * S],
                                                rws, start=start, stop=stop)

                    def attend(j):
                        pe.wait_ge(exp_ready, j + 1)
                        if j >= 2:
                            pe.wait_ge(x1_ready, j - 1)
                        with further(pe, counts, j):
                            if j:
                                pe.wait_ge(pT_copied, j)
                            pe.wait_ge(r_exp[j], 1)
                            for g in range(0, REST, 4):
                                if g:
                                    pe.wait_ge(r_copied[j], g // 4)
                                for c in range(g, min(g + 4, REST)):
                                    ins = nc.tensor.transpose(bank[:, 5, (c - g) * P:(c - g + 1) * P],
                                                              prest[:, c * P:(c + 1) * P], ident[:])
                                ins.then_inc(r_pT[j], 1)
                            pe.wait_ge(r_copied[j], -(-REST // 4))
                        if j:
                            pe.wait_ge(pT_copied, j)
                        for c in range(FEW):
                            ins = nc.tensor.transpose(bank[:, 5, c * P:(c + 1) * P], prob[:, j % 2, c * P:(c + 1) * P], ident[:])
                        ins.then_inc(pT_done, 1)
                        pe.wait_ge(pT_copied, j + 1)
                        for half in range(HB):
                            pe.wait_ge(ld_rows[j % 2][half], 16 * FEW * (j // 2 + 1))
                            sum_chunk(j, half, probT[:, j % 2, 0], cbuf[j % 2][:, half, 0, D:2 * D], True, False)
                        with further(pe, counts, j):
                            for half in range(HB):
                                pe.wait_ge(r_load[j], 16 * REST * (HB + half + 1))
                                for c in range(REST):
                                    ins = sum_chunk(j, half, prestT[:, c], crest[:, c, D:2 * D], False, False)
                                ins.then_inc(r_pv[j], 1)
                            pe.wait_ge(r_pv[j], HB)
                        for half in range(HB):
                            for c in range(1, FEW):
                                ins = sum_chunk(j, half, probT[:, j % 2, c], cbuf[j % 2][:, half, c, D:2 * D],
                                                False, c == FEW - 1)
                        ins.then_inc(pv_done, 1)

                    scores(0)
                    for j in range(NT):
                        further_scores(j)
                        if j + 1 < NT:
                            scores(j + 1)
                        attend(j)

        with ExitStack() as ph:
            def sbp(name, shape, dt=F32):
                return ph.enter_context(nc.sbuf_tensor(name, shape, dt))

            qkT = sbp("qkT", [P, 2 * NG, T])
            v = sbp("v", [P, NT, D])
            vswap = sbp("vswap", [P, NT, D])
            sc = sbp("sc", [P, 2, HEADS, S])
            pT = sbp("pT", [P, 2, HEADS // 2, P])
            o = xn
            wout_sb = sbp("wout_sb", [P, KD, D])
            oT = xT
            hmax = sbp("hmax", [P, NT, HEADS])
            hsum = sbp("hsum", [P, NT, HEADS])
            hinv = sbp("hinv", [P, NT, HEADS])

            qk_done, qk_ready = sem("qk_done"), sem("qk_ready")
            v_done, v_ready, vswap_ready = sem("v_done"), sem("v_ready"), sem("vswap_ready")
            hs_done, hs_read = sem("hs_done"), sem("hs_read")
            hmax_ready, sub_ready, hexp_ready = sem("hmax_ready"), sem("sub_ready"), sem("hexp_ready")
            hsum_ready, hinv_ready = sem("hsum_ready"), sem("hinv_ready")
            hpT_done, hpT_copied = sem("hpT_done"), sem("hpT_copied")
            ho_done, o_ready = sem("ho_done"), sem("o_ready")
            oT_done, oT_ready = sem("oT_done"), sem("oT_ready")
            y_done, x2_ready = sem("y_done"), sem("x2_ready")

            with nc.Block() as block:
                @block.sync
                def _(sp):
                    for n in range(LATE):
                        if n >= RING:
                            sp.wait_ge(ld_e[n % RING], 16)
                        sp.dma_start(places[:, n], w_expert[n]).then_inc(ld_e[n % RING], 16)
                    sp.dma_start(wout_sb[:], w_out).then_inc(ld_wf, 16)
                    sp.dma_start(wr_sb[:], w_router).then_inc(ld_wf, 16)
                    sp.dma_start(wsh_sb[:], w_shared).then_inc(ld_wf, 16)
                    for n in range(LAST):
                        sp.dma_start(last[:, n], w_expert[E - LAST + n]).then_inc(ld_wf, 16)
                    for half in range(HB):
                        sp.wait_ge(v_ready, NT)
                        lo, hi = half * S, (1 - half) * S
                        sp.dma_start(vswap[lo:lo + S], v[hi:hi + S]).then_inc(vswap_ready, 16)
                    sp.wait_ge(qk_done, 2 * NG)
                    for n in range(LATE, GROUP):
                        sp.wait_ge(ld_e[n % RING], 16)
                        sp.dma_start(places[:, n], w_expert[n]).then_inc(ld_e[n % RING], 16)

                @block.vector
                def _(vec):
                    norm_tiles(vec, 1)
                    for t in range(NT):
                        vec.wait_ge(v_done, t + 1)
                        nc.vector.tensor_copy(v[:, t], bank[:, 4 + t]).then_inc(v_ready, 1)

                    def softmax(j):
                        buf = sc[:, j % 2]
                        vec.wait_ge(hs_done, j + 1)
                        if j >= 2:
                            vec.wait_ge(hpT_done, 2 * (j - 1))
                        nc.vector.scalar_tensor_tensor(
                            out=buf.rearrange("p (r g) k -> p r g k", r=RG),
                            in0=bank[:, 0:4, 0:NG * S].rearrange("p r (g k) -> p r g k", g=NG), scalar=SC_HEAD,
                            in1=causal[:].rearrange("p (r g) k -> p r g k", r=RG), op0=ALU.mult, op1=ALU.add).then_inc(hs_read, 1)
                        vec.wait_ge(hs_read, j + 1)
                        nc.vector.tensor_reduce(hmax[:, j], buf, AX_X, ALU.max).then_inc(hmax_ready, 1)
                        vec.wait_ge(hmax_ready, j + 1)
                        nc.vector.tensor_tensor(buf, buf, hmax[:, j].unsqueeze(2).broadcast_to([P, HEADS, S]),
                                                ALU.subtract).then_inc(sub_ready, 1)

                    def finish(j):
                        vec.wait_ge(hexp_ready, j + 1)
                        nc.vector.tensor_reduce(hsum[:, j], sc[:, j % 2], AX_X, ALU.add).then_inc(hsum_ready, 1)
                        vec.wait_ge(hsum_ready, j + 1)
                        nc.vector.reciprocal(hinv[:, j], hsum[:, j]).then_inc(hinv_ready, 1)
                        vec.wait_ge(hinv_ready, j + 1)
                        vec.wait_ge(ho_done, j + 1)
                        for hh in range(2):
                            ov = o[:, j].rearrange("p (gp hh r d) -> p hh r gp d", gp=NG // 2, hh=2, r=RG)[:, hh]
                            iv = hinv[:, j].rearrange("p (r gp hh) -> p hh r gp", r=RG, hh=2)[:, hh]
                            nc.vector.tensor_tensor(
                                ov, bank[:, 6 + hh, 0:HEADS // 2 * DH].rearrange("p (r gp d) -> p r gp d", r=RG, gp=NG // 2),
                                iv.unsqueeze(3).broadcast_to([P, RG, NG // 2, DH]), ALU.mult).then_inc(o_ready, 1)

                    softmax(0)
                    for j in range(NT):
                        if j + 1 < NT:
                            softmax(j + 1)
                        finish(j)
                    for j in range(NT):
                        vec.wait_ge(y_done, j + 1)
                        nc.vector.tensor_tensor(xt[:, j], bank[:, 4 + j], xt[:, j], ALU.add).then_inc(x2_ready, 1)
                        vec.wait_ge(x2_ready, j + 1)
                        norm_stats(j)

                @block.scalar
                def _(act):
                    norm_roots(act, 1)
                    copy_turned(act, 1, 2)
                    for g in range(2 * NG):
                        act.wait_ge(qk_done, g + 1)
                        nc.scalar.activation(qkT[:, g], bank[:, g % 4], ACT.Copy).then_inc(qk_ready, 1)

                    def copies(j):
                        for n in range(2):
                            act.wait_ge(hpT_done, 2 * j + n + 1)
                            if j >= 2:
                                act.wait_ge(ho_done, j - 1)
                            nc.scalar.activation(pT[:, j % 2, 4 * n:4 * n + 4],
                                                 bank[:, 4 + n].rearrange("p (c q) -> p c q", c=4),
                                                 ACT.Copy).then_inc(hpT_copied, 1)

                    for j in range(NT):
                        act.wait_ge(sub_ready, j + 1)
                        nc.scalar.activation(sc[:, j % 2], sc[:, j % 2], ACT.Exp).then_inc(hexp_ready, 1)
                        copies(j)
                    for j in range(NT):
                        act.wait_ge(oT_done, j + 1)
                        nc.scalar.activation(oT[:, :, j * P:(j + 1) * P],
                                             bank[:, j].rearrange("p (k t) -> p k t", k=KD),
                                             ACT.Copy).then_inc(oT_ready, 1)

                @block.tensor
                def _(pe):
                    turn_tiles(pe, 1, 2)
                    pe.wait_ge(ld_w, 16 * 2)
                    for t in range(NT):
                        pe.wait_ge(xT_ready, NT + t + 1)
                        for k in range(KD):
                            ins = nc.tensor.matmul(bank[:, 4 + t], xT[:, k, t * P:(t + 1) * P],
                                                   wqkv_sb[:, k, 2 * D:3 * D], start=(k == 0), stop=(k == KD - 1))
                        ins.then_inc(v_done, 1)
                    for g in range(2 * NG):
                        if g >= 4:
                            pe.wait_ge(qk_ready, g - 3)
                        for k in range(KD):
                            ins = nc.tensor.matmul(bank[:, g % 4], wqkv_sb[:, k, g * P:(g + 1) * P], xT[:, k],
                                                   start=(k == 0), stop=(k == KD - 1))
                        ins.then_inc(qk_done, 1)

                    def scores(j):
                        if j == 0:
                            pe.wait_ge(qk_ready, 2 * NG)
                        else:
                            pe.wait_ge(hs_read, j)
                        for g in range(NG):
                            for r in range(RG):
                                rows = slice(r * DH, (r + 1) * DH)
                                for half in range(HB):
                                    tok = slice((HB * j + half) * S, (HB * j + half + 1) * S)
                                    ins = nc.tensor.matmul(bank[half * S:(half + 1) * S, r, g * S:(g + 1) * S],
                                                           qkT[rows, g, tok], qkT[rows, NG + g, tok],
                                                           start=True, stop=True, tile_position=(r * DH, half * S))
                        ins.then_inc(hs_done, 1)

                    def attend(j):
                        pe.wait_ge(hexp_ready, j + 1)
                        for n in range(2):
                            if j == 0:
                                pe.wait_ge(v_ready, NT)
                            else:
                                pe.wait_ge(hpT_copied, 2 * (j - 1) + n + 1)
                            for c in range(4):
                                tp = 4 * n + c
                                ins = nc.tensor.transpose(
                                    bank[:, 4 + n, c * P:(c + 1) * P],
                                    sc[:, j % 2, 2 * tp:2 * tp + 2].rearrange("p h k -> p (h k)"), ident[:])
                            ins.then_inc(hpT_done, 1)
                        pe.wait_ge(vswap_ready, 16 * HB)
                        if j:
                            pe.wait_ge(o_ready, 2 * j)
                        for n in range(2):
                            pe.wait_ge(hpT_copied, 2 * j + n + 1)
                            for c in range(4):
                                tp = 4 * n + c
                                r, gp = tp // (NG // 2), tp % (NG // 2)
                                for hh in range(2):
                                    h = RG * (2 * gp + hh) + r
                                    for half in range(HB):
                                        vv = v if half == hh else vswap
                                        ins = nc.tensor.matmul(
                                            bank[half * S:(half + 1) * S, 6 + hh, tp * DH:(tp + 1) * DH],
                                            pT[hh * S:(hh + 1) * S, j % 2, tp, half * S:(half + 1) * S],
                                            vv[hh * S:(hh + 1) * S, j, h * DH:(h + 1) * DH],
                                            start=True, stop=True, tile_position=(hh * S, half * S))
                        ins.then_inc(ho_done, 1)

                    scores(0)
                    for j in range(NT):
                        if j + 1 < NT:
                            scores(j + 1)
                        attend(j)
                    pe.wait_ge(hs_read, NT)
                    for j in range(NT):
                        pe.wait_ge(o_ready, 2 * (j + 1))
                        for k in range(KD):
                            ins = nc.tensor.transpose(bank[:, j, k * P:(k + 1) * P],
                                                      o[:, j, k * P:(k + 1) * P], ident[:])
                        ins.then_inc(oT_done, 1)
                    pe.wait_ge(ld_wf, 16 * (3 + LAST))
                    for j in range(NT):
                        pe.wait_ge(oT_ready, j + 1)
                        for k in range(KD):
                            ins = nc.tensor.matmul(bank[:, 4 + j], oT[:, k, j * P:(j + 1) * P], wout_sb[:, k],
                                                   start=(k == 0), stop=(k == KD - 1))
                        ins.then_inc(y_done, 1)

        early.close()
        gpos = sb("gpos", [P, NT, E])
        jtab = sb("jtab", [P, ITEMS])
        slot_no = sb("slot_no", [P, P], BF16)
        gathered = sb("gathered", [P, GB, D])
        info = sb("info", [P, NT, E, NCOL], BF16)
        sgate = sb("sgate", [P, NT])
        ssil = sb("ssil", [P, T])
        tokens_of = sb("tokens_of", [1, E], I32)
        over_e = sb("over_e", [1, OVER], I32)
        over_more = sb("over_more", [1, 1], I32)
        with ExitStack() as ph:
            def sbp(name, shape, dt=F32):
                return ph.enter_context(nc.sbuf_tensor(name, shape, dt))

            logit = sbp("logit", [P, NT, EO])
            top8 = sbp("top8", [P, NT, 8])
            rest = sbp("rest", [P, NT, E])
            chosen = sbp("chosen", [P, NT, E])
            chosen_b = sbp("chosen_b", [P, NT, E], BF16)
            chosenT = sbp("chosenT", [E, NT, P], BF16)
            lexp = sbp("lexp", [P, NT, E])
            nl = sbp("nl", [P, NT])
            wsum = sbp("wsum", [P, NT])
            winv = sbp("winv", [P, NT])
            comb = sbp("comb", [P, NT, E])
            left = sbp("left", [P, 2, NT, E])
            pos = sbp("pos", [P, NT, E])
            g1 = sbp("g1", [P, NT, E])
            g2 = sbp("g2", [P, NT, E])
            tri = sbp("tri", [P, P], BF16)
            ones = sbp("ones", [P, P], BF16)
            ident_b = sbp("ident_b", [P, P], BF16)
            ci = sbp("ci", [P, ITEMS], I32)
            cp = sbp("cp", [P, 1], I32)
            cpf = sbp("cpf", [P, 1])
            ce = sbp("ce", [P, E])
            cover = sbp("cover", [P, E])
            ctile = sbp("ctile", [P, NT])
            cnt = sbp("cnt", [E, 1])
            ovc = sbp("ovc", [E, MORE + 1])
            ovb = sbp("ovb", [E, P], BF16)
            cum = sbp("cum", [P, E + 1])
            shift = sbp("shift", [P, E])
            ends = sbp("ends", [E, 1])
            below = sbp("below", [E, OVER], BF16)

            logit_done, logit_ready = sem("logit_done"), sem("logit_ready")
            step, lexp_ready, chosen_ready = sem("step"), sem("lexp_ready"), sem("chosen_ready")
            const, cast = sem("const"), sem("cast")
            sh_gu, sh_sil = sem("sh_gu"), sem("sh_sil")
            count_done, ovb_ready, cum_done = sem("count_done"), sem("ovb_ready"), sem("cum_done")
            pos_done, chT_done, chT_ready, rank_done = sem("pos_done"), sem("chT_done"), sem("chT_ready"), sem("rank_done")

            with nc.Block() as block:
                @block.sync
                def _(sp):
                    sp.wait_ge(xn_ready, 3 * NT)
                    sp.dma_start(tokens.rearrange("(t p) d -> p t d", p=P), xn[:]).then_inc(tokens_stored, 16)

                @block.gpsimd
                def _(pool):
                    n = 0
                    for t, pattern, base, mult in ((ci[:], [[SL, ITEMS]], 0, 0), (cp[:], [[0, 1]], 0, 1)):
                        nc.gpsimd.iota(t, pattern=pattern, base=base, channel_multiplier=mult).then_inc(const, 1)
                        n += 1
                    for t, v in ((tri, 1.0), (ones, 1.0), (ident_b, 0.0)):
                        nc.gpsimd.memset(t[:], v).then_inc(const, 1)
                        n += 1
                    pool.wait_ge(const, n)
                    nc.gpsimd.affine_select(out=tri[:], in_=tri[:], compare_op=ALU.is_gt, fill=0.0, base=0,
                                            pattern=[[1, P]], channel_multiplier=-1).then_inc(const, 1)
                    nc.gpsimd.affine_select(out=ident_b[:], in_=ident_b[:], compare_op=ALU.not_equal, fill=1.0,
                                            base=0, pattern=[[-1, P]], channel_multiplier=1).then_inc(const, 1)
                    n += 2
                    pool.wait_ge(const, n)
                    nc.gpsimd.memset(gathered[:], 0.0).then_inc(const, 1)
                    assert n + 1 == CONSTS

                @block.vector
                def _(vec):
                    norm_tiles(vec, 2)
                    vec.wait_ge(const, CONSTS)
                    nc.vector.tensor_copy(jtab[:], ci[:]).then_inc(cast, 1)
                    nc.vector.tensor_copy(cpf[:], cp[:]).then_inc(cast, 1)
                    vec.wait_ge(cast, 2)
                    nc.vector.tensor_scalar(slot_no[:, 0:ITEMS], jtab[:], 1.0 / SL, None, ALU.mult).then_inc(cast, 1)
                    nc.vector.tensor_scalar(slot_no[:, ITEMS:P], jtab[:, 0:P - ITEMS], 1.0 / SL, float(ITEMS),
                                            ALU.mult, ALU.add).then_inc(cast, 1)
                    nc.vector.tensor_scalar(ce[:], jtab[:, 0:E], 1.0, None, ALU.add).then_inc(cast, 1)
                    nc.vector.tensor_scalar(cover[:], jtab[:, 0:E], -1.0, float(SL * (E - 1)),
                                            ALU.mult, ALU.add).then_inc(cast, 1)
                    vec.wait_ge(cast, 3)
                    nc.vector.tensor_scalar(ctile[:], slot_no[:, 0:NT], float(P), -float(NONE), ALU.mult, ALU.add
                                            ).then_inc(cast, 1)
                    vec.wait_ge(cast, 7)
                    for t in range(NT):
                        nc.vector.tensor_scalar(info[:, t, :, 0], ce[:], 0.0, cpf[:, 0:1],
                                                ALU.mult, ALU.add).then_inc(cast, 1)
                        nc.vector.tensor_scalar(info[:, t, :, 1], ce[:], 0.0, ctile[:, t:t + 1],
                                                ALU.mult, ALU.add).then_inc(cast, 1)
                    vec.wait_ge(logit_done, NT)
                    nc.vector.tensor_copy(logit[:], bank[:, 6, 0:NT * EO].rearrange("p (t e) -> p t e", t=NT)
                                          ).then_inc(logit_ready, 1)
                    vec.wait_ge(logit_ready, 1)
                    for j in range(NT):
                        nc.vector.max(top8[:, j], logit[:, j, 0:E]).then_inc(step, 1)
                    vec.wait_ge(step, NT)
                    nc.vector.tensor_scalar(nl[:], top8[:, :, 0], -1.0, None, ALU.mult).then_inc(step, 1)
                    for j in range(NT):
                        nc.vector.match_replace(rest[:, j], top8[:, j], logit[:, j, 0:E], -3.0e38).then_inc(step, 1)
                    n = [2 * NT + 1]

                    def chain(ins):
                        n[0] += 1
                        ins.then_inc(step, 1)
                        vec.wait_ge(step, n[0])

                    vec.wait_ge(step, n[0])
                    nc.vector.tensor_tensor(chosen_b[:], rest[:], logit[:, :, 0:E], ALU.not_equal
                                            ).then_inc(chosen_ready, 1)
                    nc.vector.tensor_tensor(chosen[:], rest[:], logit[:, :, 0:E], ALU.not_equal
                                            ).then_inc(chosen_ready, 1)
                    vec.wait_ge(chosen_ready, 2)
                    vec.wait_ge(lexp_ready, NT)
                    chain(nc.vector.tensor_tensor(lexp[:], chosen[:], lexp[:], ALU.mult))
                    chain(nc.vector.tensor_reduce(wsum[:], lexp[:], AX_X, ALU.add))
                    chain(nc.vector.reciprocal(winv[:], wsum[:]))
                    chain(nc.vector.tensor_tensor(comb[:], lexp[:], winv[:].unsqueeze(2).broadcast_to([P, NT, E]),
                                                  ALU.mult))
                    chain(nc.vector.tensor_copy(info[:, :, :, 3], comb[:]))
                    chain(nc.vector.tensor_tensor(left[:, 0], comb[:], info[:, :, :, 3], ALU.subtract))
                    chain(nc.vector.tensor_copy(info[:, :, :, 4], left[:, 0]))
                    chain(nc.vector.tensor_tensor(left[:, 1], left[:, 0], info[:, :, :, 4], ALU.subtract))
                    nc.vector.tensor_copy(info[:, :, :, 5], left[:, 1]).then_inc(cast, 1)
                    vec.wait_ge(count_done, 1)
                    nc.vector.tensor_copy(tokens_of[:], bank[0:1, 4, E:2 * E]).then_inc(cast, 1)
                    chain(nc.vector.tensor_copy(cnt[:], bank[0:E, 4, 0:1]))
                    for c in range(1, MORE + 1):
                        nc.vector.tensor_scalar(ovc[:, c:c + 1], cnt[:], float(c * SL), None, ALU.is_gt).then_inc(step, 1)
                    n[0] += MORE
                    vec.wait_ge(step, n[0])
                    chain(nc.vector.tensor_reduce(ovc[:, 0:1], ovc[:, 1:MORE + 1], AX_X, ALU.add))
                    nc.vector.tensor_copy(ovb[:], ovc[:, 0:1].broadcast_to([E, P])).then_inc(ovb_ready, 1)
                    vec.wait_ge(chT_done, 1)
                    nc.vector.tensor_copy(chosenT[:], bank[0:E, 3].rearrange("e (t p) -> e t p", t=NT)
                                          ).then_inc(chT_ready, 1)
                    vec.wait_ge(cum_done, 1)
                    chain(nc.vector.tensor_copy(cum[:], bank[:, 5, 0:E + 1]))
                    chain(nc.vector.tensor_copy(ends[:], bank[0:E, 5, 128:129]))
                    nc.vector.tensor_scalar(below[:], slot_no[0:E, 0:OVER], ends[:, 0:1], None, ALU.is_ge
                                            ).then_inc(ovb_ready, 1)
                    vec.wait_ge(pos_done, 1)
                    chain(nc.vector.tensor_copy(pos[:], bank[:, 2, 0:NT * E].rearrange("p (t e) -> p t e", t=NT)))
                    chain(nc.vector.scalar_tensor_tensor(out=shift[:], in0=cum[:, 0:E], scalar=float(SL), in1=cover[:],
                                                         op0=ALU.mult, op1=ALU.add))
                    chain(nc.vector.scalar_tensor_tensor(out=g1[:], in0=pos[:], scalar=float(SL),
                                                         in1=shift[:].unsqueeze(1).broadcast_to([P, NT, E]),
                                                         op0=ALU.is_ge, op1=ALU.mult))
                    chain(nc.vector.tensor_tensor(g2[:], pos[:], ce[:].unsqueeze(1).broadcast_to([P, NT, E]), ALU.add))
                    chain(nc.vector.tensor_tensor(g1[:], g1[:], g2[:], ALU.add))
                    chain(nc.vector.tensor_tensor(g2[:], g1[:], chosen[:], ALU.mult))
                    chain(nc.vector.tensor_scalar(gpos[:], g2[:], -1.0, None, ALU.add))
                    vec.wait_ge(rank_done, 2)
                    nc.vector.tensor_scalar(over_e[:], bank[0:1, 5, 256:256 + OVER], float(E - 1), None, ALU.min
                                            ).then_inc(cast, 1)
                    nc.vector.tensor_scalar(over_more[:], cum[0:1, E:E + 1], 1.0, -1.0, ALU.max, ALU.add).then_inc(cast, 1)
                    vec.wait_ge(rank_done, 1)
                    for t in range(NT):
                        nc.vector.tensor_scalar(info[:, t, :, 2], bank[:, 1, t * E:(t + 1) * E], float(T), ctile[:, t:t + 1],
                                                ALU.mult, ALU.add).then_inc(cast, 1)

                @block.scalar
                def _(act):
                    norm_roots(act, 2)
                    copy_turned(act, 2, 2)
                    act.wait_ge(step, NT + 1)
                    for j in range(NT):
                        nc.scalar.activation(lexp[:, j], logit[:, j, 0:E], ACT.Exp,
                                             bias=nl[:, j:j + 1]).then_inc(lexp_ready, 1)
                    nc.scalar.activation(sgate[:], logit[:, :, E], ACT.Sigmoid).then_inc(cast, 1)
                    act.wait_ge(sh_gu, 1)
                    nc.scalar.activation(ssil[:], bank[:, 0], ACT.Silu).then_inc(sh_sil, 1)

                @block.tensor
                def _(pe):
                    def shared(half, k):
                        return nc.tensor.matmul(bank[:, 6 * half], wsh_sb[:, (k * 2 + half) * I:(k * 2 + half + 1) * I],
                                                xT[:, k], start=(k == 0), stop=(k == KD - 1))

                    turn_tiles(pe, 2, 2)
                    pe.wait_ge(ld_wf, 16 * (3 + LAST))
                    for j in range(NT):
                        pe.wait_ge(xT_ready, 2 * NT + j + 1)
                        for k in range(KD):
                            ins = nc.tensor.matmul(bank[:, 6, j * EO:(j + 1) * EO], xT[:, k, j * P:(j + 1) * P],
                                                   wr_sb[:, k], start=(k == 0), stop=(k == KD - 1))
                        ins.then_inc(logit_done, 1)
                    for k in range(KD - 1):
                        shared(0, k)
                    pe.wait_ge(chosen_ready, 1)
                    pe.wait_ge(const, CONSTS)
                    for t in range(NT):
                        ins = nc.tensor.matmul(bank[0:E, 4, 0:1], chosen_b[:, t], ones[:, 0:1],
                                               start=(t == 0), stop=(t == NT - 1))
                    for t in range(NT):
                        ins = nc.tensor.matmul(bank[0:1, 4, E:2 * E], ones[:, 0:1], chosen_b[:, t],
                                               start=(t == 0), stop=(t == NT - 1))
                    ins.then_inc(count_done, 1)
                    for t in range(NT):
                        ins = nc.tensor.matmul(bank[0:E, 3, t * P:(t + 1) * P], chosen_b[:, t], ident_b[:],
                                               start=True, stop=True)
                    ins.then_inc(chT_done, 1)
                    for t in range(NT):
                        for u in range(t + 1):
                            ins = nc.tensor.matmul(bank[:, 2, t * E:(t + 1) * E], (tri if u == t else ones)[:],
                                                   chosen_b[:, u], start=(u == 0), stop=(u == t))
                    ins.then_inc(pos_done, 1)
                    shared(0, KD - 1).then_inc(sh_gu, 1)
                    for k in range(KD - 1):
                        shared(1, k)
                    pe.wait_ge(ovb_ready, 1)
                    nc.tensor.matmul(bank[:, 5, 0:E + 1], ovb[:], tri[0:E, 0:E + 1], start=True, stop=True)
                    nc.tensor.matmul(bank[0:E, 5, 128:129], tri[0:E, 1:E + 1], ovb[:, 0:1], start=True, stop=True
                                     ).then_inc(cum_done, 1)
                    pe.wait_ge(chT_ready, 1)
                    for t in range(NT):
                        ins = nc.tensor.matmul(bank[:, 1, t * E:(t + 1) * E], chosenT[:, t], tri[0:E, 0:E],
                                               start=True, stop=True)
                    ins.then_inc(rank_done, 1)
                    pe.wait_ge(ovb_ready, 2)
                    nc.tensor.matmul(bank[0:1, 5, 256:256 + OVER], ones[0:E, 0:1], below[:], start=True, stop=True
                                     ).then_inc(rank_done, 1)
                    shared(1, KD - 1).then_inc(sh_gu, 1)

        with ExitStack() as ph:
            def sbp(name, shape, dt=F32):
                return ph.enter_context(nc.sbuf_tensor(name, shape, dt))

            pick = sbp("pick", [P, 2, NT, SL], BF16)
            idx = sbp("idx", [SL, RING, 2], I32)
            wslot = sbp("wslot", [SL, RING])
            slotT = sbp("slotT", [P, 2, KD, SL])
            sil = sbp("sil", [P, 2, SL])
            hid = sbp("hid", [P, 2, SL])
            hid_hi, hid_lo = sbp("hid_hi", [P, 2, SL], F32R), sbp("hid_lo", [P, 2, SL], F32R)
            dn_hi, dn_lo = sbp("dn_hi", [P, DB, D], F32R), sbp("dn_lo", [P, DB, D], F32R)
            eo = sbp("eo", [SL, RING // 2, D])
            part = flat[:, 0:NT * TOP * D].rearrange("p (t k d) -> p t k d", t=NT, k=TOP)
            shid = sbp("shid", [P, T])
            total = gathered

            picked = sem("picked")
            idx_done, idx_ready = sem("idx_done"), sem("idx_ready")
            ld_g = [sem(f"ld_g{u}") for u in range(GB)]
            sT_done, sT_ready = sem("sT_done"), sem("sT_ready")
            gu_done, sil_ready, hid_ready = sem("gu_done"), sem("sil_ready"), sem("hid_ready")
            eo_done, eo_ready = sem("eo_done"), sem("eo_ready")
            st_e = [sem(f"st_e{u}") for u in range(RING // 2)]

            pool_steps = sem("pool_steps")
            dn_hi_ready, dn_ready = sem("dn_hi_ready"), sem("dn_ready")

            def item(q, m):
                return q * GROUP + m

            def fours(q, m):
                return q * (GROUP // 4) + m // 4

            def loads(q, m):
                return q * (GROUP // RING) + m // RING

            def at_least(eng, s, v):
                if not isinstance(v, int) or v > 0:
                    eng.wait_ge(s, v)

            PIPED = E + 1

            def exists(q, m):
                return not isinstance(q, int) or 0 <= item(q, m) < PIPED

            def gate_w(w, half, k):
                return w[:, (k * 2 + half) * I:(k * 2 + half + 1) * I]

            def down_w(w):
                return w[:, KD * 2 * I:WE]

            def one(n):
                return slice(n, n + 1) if isinstance(n, int) else bass.ds(n, 1)

            def column(eng, q, m):
                if isinstance(q, int) and item(q, m) == E:
                    return one(eng.value_load(over_e[0:1, 0:1], min_val=0, max_val=E - 1))
                return one(item(q, m))

            def pick_slots(b, jcol, col):
                for t in range(NT):
                    ins = nc.vector.tensor_scalar(pick[:, b, t], slot_no[:, 0:SL], jcol, gpos[:, t, col],
                                                  ALU.add, ALU.is_equal)
                return ins

            def index_products(b, col):
                for t in range(NT):
                    ins = nc.tensor.matmul(bank[0:SL, 7, 0:NCOL], pick[:, b, t], info[:, t, col].rearrange("p a c -> p (a c)"),
                                           start=(t == 0), stop=(t == NT - 1))
                return ins

            def slot_numbers(u, done):
                nc.vector.tensor_reduce(wslot[:, u:u + 1], bank[0:SL, 7, 3:NCOL], AX_X, ALU.add).then_inc(done, 1)
                nc.vector.tensor_scalar(idx[:, u], bank[0:SL, 7, 1:3], bank[0:SL, 7, 0:1], float(NONE),
                                        ALU.add, ALU.add).then_inc(done, 1)

            def gather(b, u, slots):
                return nc.gpsimd.indirect_dma_start(
                    gathered[0:slots, b], None, tokens, bass.IndirectOffsetOnAxis(ap=idx[0:slots, u, 0:1], axis=0),
                    bounds_check=T - 1, oob_is_err=False)

            def scatter(b, u, slots):
                return nc.gpsimd.indirect_dma_start(
                    rows, bass.IndirectOffsetOnAxis(ap=idx[0:slots, u, 1:2], axis=0), eo[0:slots, b], None,
                    bounds_check=TOP * T - 1, oob_is_err=False)

            def move(pool, what, b, u, n, done):
                nc.gpsimd.sem_inc(pool_steps, 1)
                if isinstance(n, int) and n >= E:
                    what(b, u, SL).then_inc(done, 16)
                    return
                few = pool.value_load(tokens_of[0:1, one(n)], min_val=0, max_val=T)
                with pool.If(few > SOME[1]):
                    what(b, u, SL).then_inc(done, 16)
                with pool.Else():
                    with pool.If(few > SOME[0]):
                        what(b, u, SOME[1]).then_inc(done, 16)
                    with pool.Else():
                        what(b, u, SOME[0]).then_inc(done, 16)

            def turn(b, g):
                for k in range(KD):
                    ins = nc.tensor.transpose(bank[:, b, k * SL:(k + 1) * SL], gathered[0:SL, g, k * P:(k + 1) * P],
                                              ident[0:SL, 0:SL])
                return ins

            def of_last(q, m):
                return isinstance(q, int) and E - LAST <= item(q, m) < E

            def place(q, m):
                return last[:, item(q, m) - E + LAST] if of_last(q, m) else places[:, m % GROUP]

            def wait_loaded(eng, q, m):
                if of_last(q, m):
                    eng.wait_ge(ld_wf, 16 * (3 + LAST))
                else:
                    eng.wait_ge(ld_e[m % RING], loads(q, m) * 16 + 16)

            def gate_up(b, w):
                for half in range(2):
                    for k in range(KD):
                        ins = nc.tensor.matmul(bank[:, 2 + b, half * SL:(half + 1) * SL], gate_w(w, half, k),
                                               slotT[:, b, k], start=(k == 0), stop=(k == KD - 1))
                return ins

            def down(b, d, lead):
                for n, (h, w) in enumerate([(hid_hi, dn_hi), (hid_hi, dn_lo), (hid_lo, dn_hi)]):
                    ins = nc.tensor.matmul(bank[0:SL, lead], h[:, b], w[:, d], start=(n == 0), stop=(n == 2))
                return ins

            def groups(eng, step, ahead):
                for m in range(-ahead, GROUP):
                    step(0, m)
                with eng.Fori(1, E // GROUP - 1) as q:
                    for m in range(GROUP):
                        step(q, m)
                for m in range(GROUP + 2):
                    step(E // GROUP - 1, m)

            with nc.Block() as block:
                @block.sync
                def _(sp):
                    def load(q, m, e):
                        sp.wait_ge(eo_done, item(q, m) - GROUP + 1)
                        sp.wait_ge(ld_e[m % RING], loads(q, m) * 16)
                        sp.dma_start(place(q, m), w_expert[e].rearrange("a p n -> p (a n)")
                                     ).then_inc(ld_e[m % RING], 16)

                    with sp.Fori(1, E // GROUP - 1) as q:
                        for m in range(GROUP):
                            load(q, m, one(item(q, m)))
                    for m in range(GROUP - LAST):
                        load(E // GROUP - 1, m, one(item(E // GROUP - 1, m)))
                    load(E // GROUP, 0, bass.ds(sp.value_load(over_e[0:1, 0:1], min_val=0, max_val=E - 1), 1))

                @block.gpsimd
                def _(pool):
                    pool.wait_ge(tokens_stored, 16)

                    def step(q, m):
                        if exists(q, m + 5):
                            n, u = item(q, m + 5), (m + 5) % RING
                            pool.wait_ge(idx_ready, n * 2 + 2)
                            at_least(pool, sT_done, n - GB + 1)
                            move(pool, gather, u % GB, u, n, ld_g[u % GB])
                        if exists(q, m - 1):
                            n, u = item(q, m - 1), (m - 1) % RING
                            pool.wait_ge(eo_ready, n + 1)
                            move(pool, scatter, u % EB, u, n, st_e[u % EB])

                    groups(pool, step, 6)
                    for b in range(EB):
                        pool.wait_ge(st_e[b], 16 * -(-(PIPED - b) // EB))

                @block.vector
                def _(vec):
                    def step(q, m):
                        if exists(q, m):
                            n, u = item(q, m), m % RING
                            vec.wait_ge(sil_ready, n + 1)
                            at_least(vec, eo_done, n - 1)
                            nc.vector.tensor_tensor(hid[:, u % 2], sil[:, u % 2], bank[:, 2 + u % 2, SL:2 * SL],
                                                    ALU.mult).then_inc(hid_ready, 1)
                            vec.wait_ge(hid_ready, n * 3 + 1)
                            nc.vector.tensor_copy(hid_hi[:, u % 2], hid[:, u % 2]).then_inc(hid_ready, 1)
                            vec.wait_ge(hid_ready, n * 3 + 2)
                            nc.vector.tensor_tensor(hid_lo[:, u % 2], hid[:, u % 2], hid_hi[:, u % 2], ALU.subtract
                                                    ).then_inc(hid_ready, 1)
                        if exists(q, m + 1):
                            n, u = item(q, m + 1), (m + 1) % RING
                            vec.wait_ge(dn_hi_ready, n + 1)
                            nc.vector.tensor_tensor(dn_lo[:, u % DB], down_w(place(q, m + 1)), dn_hi[:, u % DB], ALU.subtract
                                                    ).then_inc(dn_ready, 1)
                        if exists(q, m + 5):
                            n, u = item(q, m + 5), (m + 5) % RING
                            vec.wait_ge(idx_done, n + 1)
                            at_least(vec, st_e[u % EB], fours(q, m + 5) * 16 - 16)
                            slot_numbers(u, idx_ready)
                        if exists(q, m + 6):
                            n, u = item(q, m + 6), (m + 6) % RING
                            at_least(vec, idx_done, n - 1)
                            pick_slots(u % 2, jtab[:, one(n)], column(vec, q, m + 6)).then_inc(picked, 1)

                    groups(vec, step, 6)

                @block.scalar
                def _(act):
                    def step(q, m):
                        if exists(q, m + 1):
                            n, u = item(q, m + 1), (m + 1) % RING
                            wait_loaded(act, q, m + 1)
                            at_least(act, eo_done, n - DB + 1)
                            nc.scalar.activation(dn_hi[:, u % DB], down_w(place(q, m + 1)), ACT.Copy).then_inc(dn_hi_ready, 1)
                        if exists(q, m):
                            n, u = item(q, m), m % RING
                            act.wait_ge(gu_done, n + 1)
                            at_least(act, hid_ready, n * 3 - 5)
                            nc.scalar.activation(sil[:, u % 2], bank[:, 2 + u % 2, 0:SL], ACT.Silu).then_inc(sil_ready, 1)
                        if exists(q, m - 1):
                            n, u = item(q, m - 1), (m - 1) % RING
                            act.wait_ge(eo_done, n + 1)
                            at_least(act, st_e[u % EB], fours(q, m - 1) * 16)
                            nc.scalar.activation(eo[:, u % EB], bank[0:SL, 4 + u % 2], ACT.Copy,
                                                 scale=wslot[:, u:u + 1]).then_inc(eo_ready, 1)
                        if exists(q, m + 2):
                            n, u = item(q, m + 2), (m + 2) % RING
                            act.wait_ge(sT_done, n + 1)
                            at_least(act, gu_done, n - 1)
                            nc.scalar.activation(slotT[:, u % 2], bank[:, u % 2, 0:KD * SL].rearrange("p (k s) -> p k s", k=KD),
                                                 ACT.Copy).then_inc(sT_ready, 1)

                    groups(act, step, 2)

                @block.tensor
                def _(pe):
                    def step(q, m):
                        if exists(q, m):
                            n, u = item(q, m), m % RING
                            pe.wait_ge(sT_ready, n + 1)
                            wait_loaded(pe, q, m)
                            at_least(pe, hid_ready, n * 3 - 5)
                            gate_up(u % 2, place(q, m)).then_inc(gu_done, 1)
                        if exists(q, m - 1):
                            n, u = item(q, m - 1), (m - 1) % RING
                            pe.wait_ge(hid_ready, n * 3 + 3)
                            pe.wait_ge(dn_ready, n + 1)
                            at_least(pe, eo_ready, n - 1)
                            down(u % 2, u % DB, 4 + u % 2).then_inc(eo_done, 1)
                        if exists(q, m + 2):
                            n, u = item(q, m + 2), (m + 2) % RING
                            pe.wait_ge(ld_g[u % GB], fours(q, m + 2) * 16 + 16)
                            at_least(pe, sT_ready, n - 1)
                            turn(u % 2, u % GB).then_inc(sT_done, 1)
                        if exists(q, m + 5):
                            n, u = item(q, m + 5), (m + 5) % RING
                            pe.wait_ge(picked, n + 1)
                            at_least(pe, idx_ready, n * 2)
                            index_products(u % 2, column(pe, q, m + 5)).then_inc(idx_done, 1)

                    groups(pe, step, 6)

            ov_load, ov_picked, ov_idx_done = sem("ov_load"), sem("ov_picked"), sem("ov_idx_done")
            ov_idx, ov_gathered, ov_turned = sem("ov_idx"), sem("ov_gathered"), sem("ov_turned")
            ov_sT, ov_gu, ov_sil, ov_hid = sem("ov_sT"), sem("ov_gu"), sem("ov_sil"), sem("ov_hid")
            ov_out, ov_scaled, ov_stored = sem("ov_out"), sem("ov_scaled"), sem("ov_stored")
            sp_steps, ld_soon = sem("sp_steps"), sem("ld_soon")
            PE_ROWS = 4
            sh_hid, sh_out = sem("sh_hid"), sem("sh_out")
            ld_p = [sem(f"ld_p{t}") for t in range(NT)]
            sh_added, summed, y_ready, y_stored = sem("sh_added"), sem("summed"), sem("y_ready"), sem("y_stored")

            def overflow_items(eng, more, step, after=None):
                with eng.If(more > 0):
                    step(1)
                    with eng.If(more > 1):
                        with eng.Fori(2, more + 1) as o:
                            step(o)
                    if after:
                        after()

            with nc.Block() as block:
                @block.sync
                def _(sp):
                    more = sp.value_load(over_more[0:1, 0:1], min_val=0, max_val=OVER - 1)

                    def step(o):
                        e = sp.value_load(over_e[0:1, one(o)], min_val=0, max_val=E - 1)
                        sp.wait_ge(ov_picked, o)
                        sp.dma_start(places[:, 0], w_expert[bass.ds(e, 1)].rearrange("a p n -> p (a n)")
                                     ).then_inc(ov_load, 16)

                    def all_stored():
                        sp.wait_ge(ov_stored, more * 16)
                        nc.sync.sem_inc(sp_steps, 1)

                    overflow_items(sp, more, step, all_stored)
                    rows_of = rows.rearrange("(k t p) d -> t p k d", k=TOP, t=NT)
                    for t in range(NT):
                        first = ld_soon if t == NT - 1 else ld_p[t]
                        sp.dma_start(part[:, t, 0:PE_ROWS], rows_of[t, :, 0:PE_ROWS]).then_inc(first, 16)
                        sp.dma_start(part[:, t, PE_ROWS:TOP], rows_of[t, :, PE_ROWS:TOP]).then_inc(ld_p[t], 16)
                    for t in range(NT):
                        sp.wait_ge(y_ready, t + 1)
                        sp.dma_start(out[t * P:(t + 1) * P], total[:, t]).then_inc(y_stored, 16)
                    sp.wait_ge(y_stored, 16 * NT)

                @block.gpsimd
                def _(pool):
                    more = pool.value_load(over_more[0:1, 0:1], min_val=0, max_val=OVER - 1)

                    def step(o):
                        pool.wait_ge(ov_idx, o * 2)
                        move(pool, gather, 0, 0, E, ov_gathered)
                        pool.wait_ge(ov_scaled, o)
                        move(pool, scatter, 0, 0, E, ov_stored)

                    overflow_items(pool, more, step)

                @block.vector
                def _(vec):
                    more = vec.value_load(over_more[0:1, 0:1], min_val=0, max_val=OVER - 1)

                    def step(o):
                        e = vec.value_load(over_e[0:1, one(o)], min_val=0, max_val=E - 1)
                        at_least(vec, ov_stored, o * 16 - 16)
                        pick_slots(0, jtab[:, one(o + E)], bass.ds(e, 1)).then_inc(ov_picked, 1)
                        vec.wait_ge(ov_idx_done, o)
                        slot_numbers(0, ov_idx)
                        vec.wait_ge(ov_turned, o)
                        nc.vector.tensor_copy(slotT[:, 0], bank[:, 0, 0:KD * SL].rearrange("p (k s) -> p k s", k=KD)
                                              ).then_inc(ov_sT, 1)
                        vec.wait_ge(ov_sil, o)
                        nc.vector.tensor_tensor(hid[:, 0], sil[:, 0], bank[:, 2, SL:2 * SL], ALU.mult).then_inc(ov_hid, 1)

                    overflow_items(vec, more, step)
                    vec.wait_ge(sh_sil, 1)
                    vec.wait_ge(sh_gu, 2)
                    nc.vector.tensor_tensor(shid[:], ssil[:], bank[:, 6], ALU.mult).then_inc(sh_hid, 1)
                    for t in range(NT):
                        vec.wait_ge(sh_out, t + 1)
                        nc.vector.scalar_tensor_tensor(out=xt[:, t], in0=bank[:, 4 + t], scalar=sgate[:, t:t + 1],
                                                       in1=xt[:, t], op0=ALU.mult, op1=ALU.add).then_inc(sh_added, 1)
                    for t in range(NT):
                        vec.wait_ge(ld_p[t], 16 if t == NT - 1 else 32)
                        nc.vector.tensor_reduce(xn[:, t], part[:, t, PE_ROWS:TOP].rearrange("p k d -> p d k"), AX_X, ALU.add
                                                ).then_inc(summed, 1)
                        vec.wait_ge(summed, 2 * t + 1)
                        vec.wait_ge(sh_added, t + 1)
                        nc.vector.tensor_tensor(xn[:, t], xn[:, t], xt[:, t], ALU.add).then_inc(summed, 1)
                        vec.wait_ge(summed, 2 * t + 2)
                        vec.wait_ge(sh_out, NT + t + 1)
                        nc.vector.tensor_tensor(total[:, t], xn[:, t], bank[:, t % 2], ALU.add).then_inc(y_ready, 1)

                @block.scalar
                def _(act):
                    more = act.value_load(over_more[0:1, 0:1], min_val=0, max_val=OVER - 1)

                    def step(o):
                        act.wait_ge(ov_gu, o)
                        nc.scalar.activation(sil[:, 0], bank[:, 2, 0:SL], ACT.Silu).then_inc(ov_sil, 1)
                        at_least(act, ov_stored, o * 16 - 16)
                        act.wait_ge(ov_out, o)
                        nc.scalar.activation(eo[:, 0], bank[0:SL, 4], ACT.Copy, scale=wslot[:, 0:1]).then_inc(ov_scaled, 1)

                    overflow_items(act, more, step)

                @block.tensor
                def _(pe):
                    more = pe.value_load(over_more[0:1, 0:1], min_val=0, max_val=OVER - 1)

                    def step(o):
                        e = pe.value_load(over_e[0:1, one(o)], min_val=0, max_val=E - 1)
                        pe.wait_ge(ov_picked, o)
                        index_products(0, bass.ds(e, 1)).then_inc(ov_idx_done, 1)
                        pe.wait_ge(ov_gathered, o * 16)
                        turn(0, 0).then_inc(ov_turned, 1)
                        pe.wait_ge(ov_sT, o)
                        pe.wait_ge(ov_load, o * 16)
                        gate_up(0, places[:, 0]).then_inc(ov_gu, 1)
                        pe.wait_ge(ov_hid, o)
                        nc.tensor.matmul(bank[0:SL, 4], hid[:, 0], down_w(places[:, 0]),
                                         start=True, stop=True).then_inc(ov_out, 1)

                    overflow_items(pe, more, step, lambda: pe.wait_ge(ov_scaled, more))
                    pe.wait_ge(sh_hid, 1)
                    for t in range(NT):
                        nc.tensor.matmul(bank[:, 4 + t], shid[:, t * P:(t + 1) * P], down_w(wsh_sb),
                                         start=True, stop=True).then_inc(sh_out, 1)
                    for t in range(NT):
                        if t == NT - 1:
                            pe.wait_ge(ld_soon, 16)
                        else:
                            pe.wait_ge(ld_p[t], 32)
                        if t >= 2:
                            pe.wait_ge(y_ready, t - 1)
                        for k in range(PE_ROWS):
                            ins = nc.tensor.matmul(bank[:, t % 2], ident[:], part[:, t, k],
                                                   start=(k == 0), stop=(k == PE_ROWS - 1))
                        ins.then_inc(sh_out, 1)


def kernel(**inputs):
    import numpy as np
    import concourse.bacc as bacc
    from concourse.bass_utils import run_bass_kernel_spmd

    a = {k: np.asarray(v) for k, v in inputs.items()}
    x = a["x"].reshape(-1, a["x"].shape[-1])
    D = x.shape[1]
    KD = D // P
    ctx = a["ctx_2048"]
    B, L, _ = ctx.shape
    NCH = -(-L // P)
    rows = np.zeros((B, NCH * P, D), ctx.dtype)
    rows[:, :L] = ctx
    rows = rows.reshape(B * NCH, P, D)
    cols = rows.reshape(B * NCH, P, KD, P).transpose(0, 3, 2, 1).reshape(B * NCH, P, KD * P)
    mask = np.zeros((B, NCH * P), np.bool_)
    mask[:, :L] = a["mask_BxS2_bk0"]
    bi, ci = np.divmod(np.arange(B * NCH), NCH)
    same = bi[:, None] == bi[None, :]
    consts = np.concatenate([
        same & (ci[:, None] < ci[None, :]),
        same,
        np.where(same, ci[None, :], -1),
        (bi[:, None] % HB) == (np.arange(P)[None, :] // S),
        (bi[:, None] // HB) == np.arange(B // HB)[None, :],
        bi[:, None] == np.arange(B)[None, :],
        np.arange(B * NCH)[:, None],
        ci[:, None],
    ], axis=1).astype(np.float32)

    def by_k(w):
        return w.reshape(KD, P, -1).transpose(1, 0, 2)

    def gated(gate_up, down):
        lead = gate_up.shape[:-2]
        g = gate_up.reshape(*lead, 2, P, KD, P)
        n = len(lead)
        g = g.transpose(*range(n), n + 3, n + 2, n, n + 1).reshape(*lead, P, KD * 2 * P)
        return np.concatenate([g, np.swapaxes(down, -1, -2)], axis=-1)

    arrays = {
        "x": x, "ctx_both": np.concatenate([cols, rows], axis=2), "mask": mask.reshape(B * NCH, P), "consts": consts,
        "w_qkv": by_k(a["L0_attn_w_qkv"]), "w_out": by_k(a["L0_attn_w_out"]),
        "w_router": by_k(np.concatenate([a["L0_ffn_router_w"], a["L0_ffn_shared_expert_gate_w"]], axis=0).T),
        "w_shared": gated(np.concatenate([a["L0_ffn_shared_gate_w"], a["L0_ffn_shared_up_w"]], axis=0),
                          a["L0_ffn_shared_down_w"]),
        "w_expert": gated(a["L0_ffn_gate_up_proj"], a["L0_ffn_down_proj"]),
    }
    nc = bacc.Bacc("TRN2", target_bir_lowering=False, num_devices=1)
    given, args = {}, []
    for name, arr in arrays.items():
        arr = np.ascontiguousarray(arr)
        given[f"in_{name}"] = arr
        args.append(nc.dram_tensor(f"in_{name}", arr.shape, mybir.dt.from_np(arr.dtype), kind="ExternalInput").ap())
    args.append(nc.dram_tensor("out_y", x.shape, F32, kind="ExternalOutput").ap())
    args.append(nc.dram_tensor("tokens", x.shape, F32, kind="Internal").ap())
    args.append(nc.dram_tensor("rows", (8 * x.shape[0], D), F32, kind="Internal").ap())
    build_program(nc, *args)
    res = run_bass_kernel_spmd(nc, [given], core_ids=[0])
    return res.results[0]["out_y"].reshape(a["x"].shape)
```
